# Optimizing a Trainium2 kernel written in Bass

```python
import numpy as np
import jax
import jax.numpy as jnp

def _softmax(x, axis=-1):
    return jax.nn.softmax(x, axis=axis)

def _gelu(x):
    return jax.nn.gelu(x, approximate=True)

def _silu(x):
    return jax.nn.silu(x)

def _sigmoid(x):
    return jax.nn.sigmoid(x)

def _layernorm(x, axis=-1, eps=1e-05):
    m = jnp.mean(x, axis=axis, keepdims=True)
    v = jnp.var(x, axis=axis, keepdims=True)
    return (x - m) / jnp.sqrt(v + eps)

def _scatter_add(tgt, idx, src, axis=0):
    return tgt.at[idx].add(src)

def _segment_sum(src, seg, n):
    return jax.ops.segment_sum(src, seg, n)
kernel_name = 'mk_gnn_resnorm_d4_gnn_r64_2d95d7'

def setup_inputs(seed: int=0):
    np.random.seed(seed)
    _w = jnp.asarray

    def _rec_inputs():
        import jax
        import jax.numpy as jnp
        _gk = jax.random.key(seed)
        x = -0.0003713 + 1 * jax.random.normal(jax.random.fold_in(_gk, 1), (100000, 128), jnp.float32)
        src = jax.random.randint(jax.random.fold_in(_gk, 2), (50000,), 0, 100000, jnp.int32)
        dst = jax.random.randint(jax.random.fold_in(_gk, 3), (50000,), 0, 100000, jnp.int32)
        _o = jnp.argsort(dst, stable=True)
        src = src[_o]
        dst = dst[_o]
        edge_attr_18 = 0.000237561 + 1.00007 * jax.random.normal(jax.random.fold_in(_gk, 13), (50000, 18), jnp.float32)
        edge_attr_54 = -0.000115307 + 0.999894 * jax.random.normal(jax.random.fold_in(_gk, 14), (50000, 54), jnp.float32)
        edge_weight = jax.random.uniform(jax.random.fold_in(_gk, 16), (50000,), jnp.float32, 0.0, 1)
        return (x, src, dst, edge_attr_18, edge_attr_54, edge_weight)
    x, src, dst, edge_attr_18, edge_attr_54, edge_weight = _rec_inputs()

    def _L0_gnn_setup():
        import jax, jax.numpy as jnp
        import numpy as np
        N_NODES = 100000
        N_EDGES = 25000
        C_IN = 128
        C_OUT = 128
        key = jax.random.key(seed)
        k1, k2, k3, k4, k5 = jax.random.split(key, 5)
        x = jax.random.normal(k1, (N_NODES, C_IN), dtype=jnp.float32)
        W = jax.random.normal(k2, (2 * C_IN, C_OUT), dtype=jnp.float32) * (1.0 / np.sqrt(2 * C_IN))
        b = jax.random.normal(k3, (C_OUT,), dtype=jnp.float32) * 0.01
        src = jax.random.randint(k4, (N_EDGES,), 0, N_NODES, dtype=jnp.int64 if jax.config.jax_enable_x64 else jnp.int32)
        dst = jax.random.randint(k5, (N_EDGES,), 0, N_NODES, dtype=jnp.int64 if jax.config.jax_enable_x64 else jnp.int32)
        return {'x': x, 'W': W, 'b': b, 'src': src, 'dst': dst}
    _L0_gnn_all = _L0_gnn_setup()
    _L0_gnn_in = {k: v for k, v in _L0_gnn_all.items() if k in ('W', 'b')}
    del _L0_gnn_all

    def _L1_gnn_setup():
        import jax, jax.numpy as jnp
        import numpy as np
        N, E, B = (50000, 15625, 512)
        H, MID, IN1, IN2, L, OUT = (128, 64, 54, 18, 3, 128)
        EPS = 1e-05

        def _swish(v):
            return v * jax.nn.sigmoid(v)
        key = jax.random.key(seed)
        ks = jax.random.split(key, 32)
        g = lambda k, shape: jax.random.normal(k, shape, dtype=jnp.float32) / np.sqrt(shape[-1])
        inp = {'x': jax.random.normal(ks[0], (N, H), dtype=jnp.float32), 'feature1': jax.random.normal(ks[1], (E, IN1), dtype=jnp.float32), 'feature2': jax.random.normal(ks[2], (E, IN2), dtype=jnp.float32), 'edge_index': jax.random.randint(ks[3], (2, E), 0, N), 'batch': jnp.sort(jax.random.randint(ks[4], (N,), 0, B)), 'lin_W': g(ks[5], (H, H)), 'lin_b': jnp.zeros((H,), jnp.float32), 'f1_W1': g(ks[6], (MID, IN1)), 'f1_W2': g(ks[7], (H, MID)), 'f2_W1': g(ks[8], (MID, IN2)), 'f2_W2': g(ks[9], (H, MID)), 'conv1_rel_W': g(ks[10], (H, H)), 'conv1_rel_b': jnp.zeros((H,), jnp.float32), 'conv1_root_W': g(ks[11], (H, H)), 'conv2_rel_W': g(ks[12], (H, H)), 'conv2_rel_b': jnp.zeros((H,), jnp.float32), 'conv2_root_W': g(ks[13], (H, H)), 'lin1_W': g(ks[14], (H, H)), 'lin1_b': jnp.zeros((H,), jnp.float32), 'lin2_W': g(ks[15], (H, H)), 'lin2_b': jnp.zeros((H,), jnp.float32), 'cat_W': g(ks[16], (H, 2 * H)), 'cat_b': jnp.zeros((H,), jnp.float32), 'norm_w': jnp.ones((H,), jnp.float32), 'norm_b': jnp.zeros((H,), jnp.float32), 'norm_ms': jnp.ones((H,), jnp.float32), 'lins_W': g(ks[17], (L, H, H)), 'lins_b': jnp.zeros((L, H), jnp.float32), 'final_W': g(ks[18], (OUT, H)), 'final_b': jnp.zeros((OUT,), jnp.float32)}
        return inp
    _L1_gnn_all = _L1_gnn_setup()
    _L1_gnn_in = {k: v for k, v in _L1_gnn_all.items() if k in ('lin_W', 'lin_b', 'f1_W1', 'f1_W2', 'f2_W1', 'f2_W2', 'conv1_rel_W', 'conv1_rel_b', 'conv1_root_W', 'conv2_rel_W', 'conv2_rel_b', 'conv2_root_W', 'lin1_W', 'lin1_b', 'lin2_W', 'lin2_b', 'cat_W', 'cat_b', 'norm_w', 'norm_b', 'norm_ms', 'lins_W', 'lins_b', 'final_W', 'final_b')}
    del _L1_gnn_all

    def _L2_gnn_setup():
        import jax, jax.numpy as jnp
        import numpy as np
        N = 100000
        E = 50000
        IN = 128
        OUT = 128
        key = jax.random.key(seed)
        k1, k2, k3 = jax.random.split(key, 3)
        x = jax.random.normal(k1, (N, IN), jnp.float32)
        edge_index = jax.random.randint(k2, (2, E), 0, N, dtype=jnp.int64)
        W = jax.random.normal(k3, (IN, OUT), jnp.float32) / np.sqrt(IN)
        b = jnp.zeros((OUT,), jnp.float32)
        return {'x': x, 'edge_index': edge_index, 'W': W, 'b': b}
    _L2_gnn_all = _L2_gnn_setup()
    _L2_gnn_in = {k: v for k, v in _L2_gnn_all.items() if k in ('W', 'b')}
    del _L2_gnn_all

    def _L3_gnn_setup():
        import jax, jax.numpy as jnp
        import numpy as np
        LN_EPS = 0.001
        key = jax.random.key(seed)
        k = jax.random.split(key, 6)
        N, E, F, H = (100000, 25000, 128, 128)
        x = jax.random.normal(k[0], (N, F), dtype=jnp.float32)
        edge_src = jax.random.randint(k[1], (E,), 0, N, dtype=jnp.int32)
        edge_dst = jax.random.randint(k[2], (E,), 0, N, dtype=jnp.int32)
        edge_weight = jax.random.uniform(k[3], (E,), dtype=jnp.float32)
        W = jax.random.normal(k[4], (F, H), dtype=jnp.float32) * (2.0 / F) ** 0.5
        b = jnp.zeros((H,), dtype=jnp.float32)
        gamma = jnp.ones((H,), dtype=jnp.float32)
        beta = jnp.zeros((H,), dtype=jnp.float32)
        return {'x': x, 'edge_src': edge_src, 'edge_dst': edge_dst, 'edge_weight': edge_weight, 'W': W, 'b': b, 'gamma': gamma, 'beta': beta}
    _L3_gnn_all = _L3_gnn_setup()
    _L3_gnn_in = {k: v for k, v in _L3_gnn_all.items() if k in ('W', 'b', 'gamma', 'beta')}
    del _L3_gnn_all
    return {'x': x, 'src': src, 'dst': dst, 'edge_attr_18': edge_attr_18, 'edge_attr_54': edge_attr_54, 'edge_weight': edge_weight, 'L0_gnn_W': _L0_gnn_in['W'], 'L0_gnn_b': _L0_gnn_in['b'], 'L1_gnn_lin_W': _L1_gnn_in['lin_W'], 'L1_gnn_lin_b': _L1_gnn_in['lin_b'], 'L1_gnn_f1_W1': _L1_gnn_in['f1_W1'], 'L1_gnn_f1_W2': _L1_gnn_in['f1_W2'], 'L1_gnn_f2_W1': _L1_gnn_in['f2_W1'], 'L1_gnn_f2_W2': _L1_gnn_in['f2_W2'], 'L1_gnn_conv1_rel_W': _L1_gnn_in['conv1_rel_W'], 'L1_gnn_conv1_rel_b': _L1_gnn_in['conv1_rel_b'], 'L1_gnn_conv1_root_W': _L1_gnn_in['conv1_root_W'], 'L1_gnn_conv2_rel_W': _L1_gnn_in['conv2_rel_W'], 'L1_gnn_conv2_rel_b': _L1_gnn_in['conv2_rel_b'], 'L1_gnn_conv2_root_W': _L1_gnn_in['conv2_root_W'], 'L1_gnn_lin1_W': _L1_gnn_in['lin1_W'], 'L1_gnn_lin1_b': _L1_gnn_in['lin1_b'], 'L1_gnn_lin2_W': _L1_gnn_in['lin2_W'], 'L1_gnn_lin2_b': _L1_gnn_in['lin2_b'], 'L1_gnn_cat_W': _L1_gnn_in['cat_W'], 'L1_gnn_cat_b': _L1_gnn_in['cat_b'], 'L1_gnn_norm_w': _L1_gnn_in['norm_w'], 'L1_gnn_norm_b': _L1_gnn_in['norm_b'], 'L1_gnn_norm_ms': _L1_gnn_in['norm_ms'], 'L1_gnn_lins_W': _L1_gnn_in['lins_W'], 'L1_gnn_lins_b': _L1_gnn_in['lins_b'], 'L1_gnn_final_W': _L1_gnn_in['final_W'], 'L1_gnn_final_b': _L1_gnn_in['final_b'], 'L2_gnn_W': _L2_gnn_in['W'], 'L2_gnn_b': _L2_gnn_in['b'], 'L3_gnn_W': _L3_gnn_in['W'], 'L3_gnn_b': _L3_gnn_in['b'], 'L3_gnn_gamma': _L3_gnn_in['gamma'], 'L3_gnn_beta': _L3_gnn_in['beta']}

def reference(x, src, dst, edge_attr_18, edge_attr_54, edge_weight, L0_gnn_W, L0_gnn_b, L1_gnn_lin_W, L1_gnn_lin_b, L1_gnn_f1_W1, L1_gnn_f1_W2, L1_gnn_f2_W1, L1_gnn_f2_W2, L1_gnn_conv1_rel_W, L1_gnn_conv1_rel_b, L1_gnn_conv1_root_W, L1_gnn_conv2_rel_W, L1_gnn_conv2_rel_b, L1_gnn_conv2_root_W, L1_gnn_lin1_W, L1_gnn_lin1_b, L1_gnn_lin2_W, L1_gnn_lin2_b, L1_gnn_cat_W, L1_gnn_cat_b, L1_gnn_norm_w, L1_gnn_norm_b, L1_gnn_norm_ms, L1_gnn_lins_W, L1_gnn_lins_b, L1_gnn_final_W, L1_gnn_final_b, L2_gnn_W, L2_gnn_b, L3_gnn_W, L3_gnn_b, L3_gnn_gamma, L3_gnn_beta):
    import jax
    import jax.numpy as jnp

    def _L0_gnn_ref(x, W, b, src, dst):
        import jax, jax.numpy as jnp
        import numpy as np
        N_NODES = 100000
        N_EDGES = 25000
        C_IN = 128
        C_OUT = 128
        diff = x[dst] - x[src]
        max_diff = jax.ops.segment_max(diff, dst, num_segments=x.shape[0])
        max_diff = jnp.where(jnp.isneginf(max_diff), jnp.zeros_like(max_diff), max_diff)
        h = jnp.concatenate([x, max_diff], axis=1)
        return jax.nn.relu(h @ W + b)

    def _L1_gnn_ref(x, feature1, feature2, edge_index, batch, lin_W, lin_b, f1_W1, f1_W2, f2_W1, f2_W2, conv1_rel_W, conv1_rel_b, conv1_root_W, conv2_rel_W, conv2_rel_b, conv2_root_W, lin1_W, lin1_b, lin2_W, lin2_b, cat_W, cat_b, norm_w, norm_b, norm_ms, lins_W, lins_b, final_W, final_b):
        import jax, jax.numpy as jnp
        import numpy as np
        N, E, B = (50000, 15625, 512)
        H, MID, IN1, IN2, L, OUT = (128, 64, 54, 18, 3, 128)
        EPS = 1e-05

        def _swish(v):
            return v * jax.nn.sigmoid(v)
        src, dst = (edge_index[0], edge_index[1])
        n = x.shape[0]
        x = _swish(x @ lin_W.T + lin_b)
        f1 = feature1 @ f1_W1.T @ f1_W2.T
        f2 = feature2 @ f2_W1.T @ f2_W2.T
        agg1 = jax.ops.segment_sum(f1 * x[src], dst, num_segments=n)
        h1 = agg1 @ conv1_rel_W.T + conv1_rel_b + x @ conv1_root_W.T
        h1 = _swish(h1 @ lin1_W.T + lin1_b)
        agg2 = jax.ops.segment_sum(f2 * x[src], dst, num_segments=n)
        h2 = agg2 @ conv2_rel_W.T + conv2_rel_b + x @ conv2_root_W.T
        h2 = _swish(h2 @ lin2_W.T + lin2_b)
        h = jnp.concatenate([h1, h2], axis=1) @ cat_W.T + cat_b
        h = h + x
        for i in range(lins_W.shape[0]):
            h = _swish(h @ lins_W[i].T + lins_b[i]) + h
        counts = jnp.maximum(jax.ops.segment_sum(jnp.ones((n,), h.dtype), batch, num_segments=B), 1.0)
        mean = jax.ops.segment_sum(h, batch, num_segments=B) / counts[:, None]
        hc = h - mean[batch] * norm_ms
        var = jax.ops.segment_sum(hc * hc, batch, num_segments=B) / counts[:, None]
        h = norm_w * hc / jnp.sqrt(var[batch] + EPS) + norm_b
        return h @ final_W.T + final_b

    def _L2_gnn_ref(x, edge_index, W, b):
        import jax, jax.numpy as jnp
        import numpy as np
        N = 100000
        E = 50000
        IN = 128
        OUT = 128
        n = x.shape[0]
        h = x @ W
        loops = jnp.arange(n, dtype=edge_index.dtype)
        src = jnp.concatenate([edge_index[0], loops])
        dst = jnp.concatenate([edge_index[1], loops])
        deg = jax.ops.segment_sum(jnp.ones_like(dst, dtype=x.dtype), dst, num_segments=n)
        dis = jnp.where(deg > 0, jax.lax.rsqrt(deg), 0.0)
        norm = dis[src] * dis[dst]
        msg = h[src] * norm[:, None]
        agg = jax.ops.segment_sum(msg, dst, num_segments=n)
        return jax.nn.relu(agg + b)

    def _L3_gnn_ref(x, edge_src, edge_dst, edge_weight, W, b, gamma, beta):
        import jax, jax.numpy as jnp
        import numpy as np
        LN_EPS = 0.001
        N = x.shape[0]
        h = x @ W
        msg = h[edge_src] * edge_weight[:, None]
        agg = jax.ops.segment_sum(msg, edge_dst, num_segments=N)
        y = agg + b
        mu = jnp.mean(y, axis=-1, keepdims=True)
        var = jnp.mean(jnp.square(y - mu), axis=-1, keepdims=True)
        y = (y - mu) * jax.lax.rsqrt(var + LN_EPS) * gamma + beta
        return jax.nn.relu(y)
    edge_index = jnp.stack([src, dst])
    batch0 = jnp.zeros((100000,), jnp.int32)
    x = _layernorm(x + _L0_gnn_ref(x, L0_gnn_W, L0_gnn_b, src, dst), axis=-1)
    x = _layernorm(x + _L1_gnn_ref(x, edge_attr_54, edge_attr_18, edge_index, batch0, L1_gnn_lin_W, L1_gnn_lin_b, L1_gnn_f1_W1, L1_gnn_f1_W2, L1_gnn_f2_W1, L1_gnn_f2_W2, L1_gnn_conv1_rel_W, L1_gnn_conv1_rel_b, L1_gnn_conv1_root_W, L1_gnn_conv2_rel_W, L1_gnn_conv2_rel_b, L1_gnn_conv2_root_W, L1_gnn_lin1_W, L1_gnn_lin1_b, L1_gnn_lin2_W, L1_gnn_lin2_b, L1_gnn_cat_W, L1_gnn_cat_b, L1_gnn_norm_w, L1_gnn_norm_b, L1_gnn_norm_ms, L1_gnn_lins_W, L1_gnn_lins_b, L1_gnn_final_W, L1_gnn_final_b), axis=-1)
    x = _layernorm(x + _L2_gnn_ref(x, edge_index, L2_gnn_W, L2_gnn_b), axis=-1)
    x = _layernorm(x + _L3_gnn_ref(x, src, dst, edge_weight, L3_gnn_W, L3_gnn_b, L3_gnn_gamma, L3_gnn_beta), axis=-1)
    return x

_drawn_inputs = setup_inputs


def setup_inputs(seed=0):
    import zlib

    import numpy as np

    out = dict(_drawn_inputs(seed))
    spreads = {'L1_gnn_lin_b': (0.0, 0.1),
     'L1_gnn_conv1_rel_b': (0.0, 0.298),
     'L1_gnn_conv2_rel_b': (0.0, 0.269),
     'L1_gnn_lin1_b': (0.0, 0.314),
     'L1_gnn_lin2_b': (0.0, 0.31),
     'L1_gnn_cat_b': (0.0, 0.1),
     'L1_gnn_norm_w': (1.0, 0.2),
     'L1_gnn_norm_b': (0.0, 0.1),
     'L1_gnn_norm_ms': (1.0, 0.2),
     'L1_gnn_lins_b': (0.0, 0.1),
     'L1_gnn_final_b': (0.0, 0.1),
     'L2_gnn_b': (0.0, 0.1),
     'L3_gnn_b': (0.0, 0.1),
     'L3_gnn_gamma': (1.0, 0.2),
     'L3_gnn_beta': (0.0, 0.1)}
    factors = {'L0_gnn_b': 8.0}
    for name, (base, spread) in spreads.items():
        noise = np.random.default_rng([zlib.crc32(name.encode()), seed]).standard_normal(out[name].shape)
        drawn = base * np.exp(spread * noise) if base else spread * noise
        out[name] = jnp.asarray(drawn.astype(out[name].dtype))
    for name, factor in factors.items():
        out[name] = (out[name] * factor).astype(out[name].dtype)
    return out
```

```python
import concourse.bass as bass
from concourse import mybir
from contextlib import ExitStack


F32 = mybir.dt.float32
BF16 = mybir.dt.bfloat16
I32 = mybir.dt.int32
ALU = mybir.AluOpType
ACT = mybir.ActivationFunctionType

P = 128
H = 128
G = 4
BLK = G * P
F54, F18 = 54, 18
FA = F54 + F18
MID = 64
TW = 132
SKIP = 1 << 17
PENALTY = 3.0e38
LN_EPS = 1e-5
LN3_EPS = 1e-3
GN_EPS = 1e-5


class Turn:

    def __init__(self, q, slot, unroll):
        self.q, self.slot, self.unroll = q, slot, unroll

    @property
    def b(self):
        return self.q * self.unroll + self.slot

    def back(self, lag):
        k = self.slot - lag
        return Turn(self.q + k // self.unroll, k % self.unroll, self.unroll)

    def within(self, count):
        return not isinstance(self.q, int) or 0 <= self.b < count

    def past(self, n):
        return not isinstance(self.q, int) or self.b >= n


def staggered(eng, count, unroll, peel, lag, step):
    for t in range(peel):
        step(Turn(t // unroll, t % unroll, unroll))
    with eng.Fori(peel // unroll, count // unroll) as q:
        for u in range(unroll):
            step(Turn(q, u, unroll))
    for t in range(count, count + lag):
        step(Turn(t // unroll, t % unroll, unroll))


def phase_semaphores(nc, ctx, phase):
    held = []

    def clear():
        nc.clear_and_free_semaphores(held)
        nc.all_engine_barrier()

    def sem(name):
        held.append(nc.alloc_semaphore(name=f"{phase}_{name}"))
        return held[-1]
    ctx.callback(clear)
    return sem


def first_wait(eng, sem):
    eng.wait_ge(sem, 1)


class WaitValues:

    def __init__(self, pool, phase, count):
        self.pool = pool
        self.regs = [pool.alloc_register(f"{phase}_wait{i}") for i in range(count)]

    def __call__(self, *values):
        if all(isinstance(v, int) for v in values):
            return values
        for reg, v in zip(self.regs, values):
            self.pool.reg_mov(reg, v)
        return self.regs


def build(nc, a, out, n_nodes, debug=None):
    NB = a["x"].shape[0] // BLK
    EB = a["dst_rows"].shape[0] // BLK
    LAST = n_nodes - (NB - 1) * BLK
    assert NB % 4 == 0 and EB % 2 == 0 and 0 < LAST <= BLK and LAST % G == 0
    assert NB * BLK < SKIP
    NROWS = NB * BLK

    def dram(name, shape, dt=F32):
        return nc.dram_tensor(name, shape, dt, kind="Internal").ap()

    tab = dict(
        narrow=dram("table_narrow", (NROWS, TW)), wide=dram("table_wide", (NROWS, 2 * H)),
        last=dram("table_last", (NROWS, H)), x1=dram("x1_rows", (NROWS, H)), hT=dram("hT", (NB, P, BLK)),
        y2=dram("y2", (NROWS, H)), x3=dram("x3", (NROWS, H)),
        cont=dram("cont_row", (1, EB * BLK), BF16), pen=dram("pen_row", (1, EB * BLK), BF16))

    with ExitStack() as top:
        def sb(name, shape, dt=F32):
            return top.enter_context(nc.sbuf_tensor(name, shape, dt))

        s = dict(
            mask=sb("mask", [P, EB * BLK], BF16),
            src=sb("src_cols", [P, EB * G], I32), scat=sb("scatter_cols", [P, EB * G], I32),
            ew=sb("edge_weight_cols", [P, EB * G]),
            ident=sb("ident", [P, P]), zero=sb("zero", [P, 2048]), eps=sb("eps", [P, 2]), ones=sb("ones", [1, BLK]),
            w0=sb("w0", [P, 2, H]), b0=sb("b0_row", [P, H]),
            lin=sb("lin", [P, H]), A1=sb("A1", [P, H]), R1=sb("R1", [P, H]), A2=sb("A2", [P, H]), R2=sb("R2", [P, H]),
            FW1=sb("FW1", [FA, H]), FW2=sb("FW2", [FA, H]), cat=sb("cat", [P, 2, H]), lins=sb("lins", [P, 3, H]),
            fin=sb("fin", [P, H]), finb=sb("fin_b_row", [P, H]),
            cols=sb("cols", [P, 16]), w2=sb("w2", [P, H]), b2=sb("b2_row", [P, H]), w3=sb("w3", [P, H]),
            b3=sb("b3_row", [P, H]), g3=sb("gamma_row", [P, H]), be3=sb("beta_row", [P, H]),
            default=sb("default_row", [P, G, H]),
            stats=sb("norm_stats", [P, NB, 6]), deg=sb("deg", [P, NB * G]), sdeg=sb("sqrt_deg", [P, NB * G]),
            dis=sb("dis", [P, NB * G]),
        )
        setup(nc, a, tab, s, EB, NB)
        edges0(nc, a, tab, s, EB)
        nodes0(nc, a, tab, s, NB)
        edges1(nc, a, tab, s, EB)
        nodes1(nc, tab, s, NB, LAST)
        norm1(nc, tab, s, NB)
        edges2(nc, tab, s, EB)
        nodes2(nc, tab, s, NB)
        edges3(nc, tab, s, EB)
        nodes3(nc, tab, s, out, NB, LAST)


LIN_B, B1, B2, CAT_B, LS0, LS1, LS2, REL1B, REL2B, L1B, L2B, NORM_W, NORM_B, NORM_MS = range(14)


def setup(nc, a, tab, s, EB, NB):
    with ExitStack() as ctx:
        def sb(name, shape, dt=F32):
            return ctx.enter_context(nc.sbuf_tensor(name, shape, dt))

        sem = phase_semaphores(nc, ctx, "setup")

        dst = sb("dst_cols", [P, EB * G], I32)
        nxt = sb("next_cols", [P, EB * G], I32)
        same = sb("same_as_next", [P, EB * G])
        dst_r = sb("dst_rows", [P, EB * G], I32)
        prv_r = sb("prev_rows", [P, EB * G], I32)
        cont = sb("cont_f32", [P, EB * G])
        cont16 = sb("cont_bf16", [P, EB * G], BF16)
        pen16 = sb("pen_bf16", [P, EB * G], BF16)
        f1w1 = sb("f1w1", [MID, FA])
        f2w1 = sb("f2w1", [MID, FA])
        f1w2, f2w2 = sb("f1w2", [MID, H]), sb("f2w2", [MID, H])
        rel1, root1, rel2, root2 = (sb(n, [P, H]) for n in ("rel1", "root1", "rel2", "root2"))
        lin1, lin2 = sb("lin1", [P, H]), sb("lin2", [P, H])
        d_st, d_mv, d_sd, d_rs = sb("d_st", [P, 6]), sb("d_mv", [P, 2]), sb("d_sd", [P, 1]), sb("d_rs", [P, 1])
        row = sb("row", [P, H])
        ps_w = ctx.enter_context(nc.psum_tensor("ps_w", [P, 4, H], F32))
        ps_f = ctx.enter_context(nc.psum_tensor("ps_f", [FA, 2, H], F32))
        ps_b = ctx.enter_context(nc.psum_tensor("ps_b", [P, 2], F32))

        idx_loaded, mask_loaded, weights_loaded = sem("idx_loaded"), sem("mask_loaded"), sem("weights_loaded")
        pads_cleared, pad_weights = sem("pads_cleared"), sem("pad_weights")
        zeroed, consts, masks, masks_stored, pen_in = (
            sem(n) for n in ("zeroed", "consts", "masks", "masks_stored", "pen_in"))
        table_zeroed, products, chain, std_ready = (
            sem(n) for n in ("table_zeroed", "products", "chain", "std_ready"))

        def col(v):
            return v.rearrange("(p o) -> p o", o=1)

        def row_to_all(v):
            return v.rearrange("(o n) -> o n", o=1).broadcast_to([P, H])

        col_loads = [(LIN_B, "L1_gnn_lin_b"), (CAT_B, "L1_gnn_cat_b"), (REL1B, "L1_gnn_conv1_rel_b"),
                     (REL2B, "L1_gnn_conv2_rel_b"), (L1B, "L1_gnn_lin1_b"), (L2B, "L1_gnn_lin2_b"),
                     (NORM_W, "L1_gnn_norm_w"), (NORM_B, "L1_gnn_norm_b"), (NORM_MS, "L1_gnn_norm_ms")]
        loads = [(s["w0"][:, :, :], a["L0_gnn_W"].rearrange("(s k) o -> k s o", s=2)),
                 (s["lin"][:, :], a["lin_T"]), (s["cat"][:, :, :], a["cat_T"].rearrange("(s k) o -> k s o", s=2)),
                 (s["fin"][:, :], a["final_T"]), (s["w2"][:, :], a["L2_gnn_W"]), (s["w3"][:, :], a["L3_gnn_W"]),
                 (rel1[:, :], a["L1_gnn_conv1_rel_W"]), (root1[:, :], a["L1_gnn_conv1_root_W"]),
                 (rel2[:, :], a["L1_gnn_conv2_rel_W"]), (root2[:, :], a["L1_gnn_conv2_root_W"]),
                 (lin1[:, :], a["lin1_T"]), (lin2[:, :], a["lin2_T"]),
                 (f1w2[:, :], a["f1_W2_T"]), (f2w2[:, :], a["f2_W2_T"]),
                 (s["lins"][:, :, :], a["lins_T"].rearrange("l k m -> k l m")),
                 (s["cols"][:, LS0:LS2 + 1], a["lins_b_T"]),
                 (s["b0"][:, :], row_to_all(a["L0_gnn_b"])), (s["finb"][:, :], row_to_all(a["L1_gnn_final_b"])),
                 (s["b2"][:, :], row_to_all(a["L2_gnn_b"])), (s["b3"][:, :], row_to_all(a["L3_gnn_b"])),
                 (s["g3"][:, :], row_to_all(a["L3_gnn_gamma"])), (s["be3"][:, :], row_to_all(a["L3_gnn_beta"]))]
        loads += [(s["cols"][:, c:c + 1], col(a[n])) for c, n in col_loads]

        block = ctx.enter_context(nc.Block())

        @block.sync
        def _(sp):
            for dst_ap, v in ((dst_r, "dst_rows"), (prv_r, "prev_rows")):
                sp.dma_start(dst_ap[:, :], a[v].rearrange("(p t) -> p t", p=P)).then_inc(mask_loaded, 16)
            sp.wait_ge(zeroed, 1)
            flat = tab["narrow"].rearrange("(p r) c -> p (r c)", p=P)
            width = flat.shape[1]
            step = 1980
            for c in range(0, width, step):
                w = min(step, width - c)
                sp.dma_start(flat[:, c:c + w], s["zero"][:, 0:w]).then_inc(table_zeroed, 16)
            n = -(-width // step)
            sp.wait_ge(table_zeroed, 16 * n)

        @block.scalar
        def _(act):
            for dst_ap, v in ((dst, "dst_cols"), (nxt, "next_cols"), (s["src"], "src_cols")):
                act.dma_start(dst_ap[:, :], a[v]).then_inc(idx_loaded, 16)
            act.dma_start(s["ew"][:, :], a["edge_weight_cols"]).then_inc(idx_loaded, 16)
            for d, v in loads:
                act.dma_start(d, v).then_inc(weights_loaded, 16)
            act.wait_ge(pads_cleared, 2)
            act.dma_start(f1w1[:, 0:F54], a["L1_gnn_f1_W1"]).then_inc(pad_weights, 16)
            act.dma_start(f2w1[:, F54:FA], a["L1_gnn_f2_W1"]).then_inc(pad_weights, 16)
            act.wait_ge(masks, 3)
            act.dma_start(tab["cont"].rearrange("o (p t) -> (o p) t", p=P), cont16[:, :]).then_inc(masks_stored, 16)
            act.dma_start(tab["pen"].rearrange("o (p t) -> (o p) t", p=P), pen16[:, :]).then_inc(masks_stored, 16)
            act.wait_ge(masks_stored, 32)
            act.dma_start(s["mask"][:, :], tab["pen"].broadcast_to([P, EB * BLK]),
                          max_dma_last_dim=16384).then_inc(pen_in, 16)
            act.wait_ge(chain, 2)
            act.wait_ge(consts, 6)
            nc.scalar.activation(d_sd[:, :], d_mv[:, 1:2], ACT.Sqrt, bias=s["eps"][:, 1:2]).then_inc(std_ready, 1)
            act.wait_ge(idx_loaded, 64)
            act.wait_ge(pen_in, 16)

        @block.gpsimd
        def _(pool):
            nc.gpsimd.memset(s["zero"][:, :], 0.0).then_inc(zeroed, 1)
            nc.gpsimd.memset(f1w1[:, :], 0.0).then_inc(pads_cleared, 1)
            nc.gpsimd.memset(f2w1[:, :], 0.0).then_inc(pads_cleared, 1)
            nc.gpsimd.memset(s["ident"][:, :], 0.0).then_inc(consts, 1)
            nc.gpsimd.memset(s["eps"][:, 0:1], LN_EPS).then_inc(consts, 1)
            nc.gpsimd.memset(s["eps"][:, 1:2], LN3_EPS).then_inc(consts, 1)
            nc.gpsimd.memset(s["ones"][:, :], 1.0).then_inc(consts, 1)
            nc.gpsimd.memset(s["cols"][:, 14:16], 0.0).then_inc(consts, 1)
            pool.wait_ge(consts, 5)
            nc.gpsimd.affine_select(out=s["ident"][:, :], in_=s["ident"][:, :], compare_op=ALU.not_equal, fill=1.0,
                                    base=0, pattern=[[-1, P]], channel_multiplier=1).then_inc(consts, 1)

        @block.tensor
        def _(pe):
            pe.wait_ge(weights_loaded, 16 * len(loads))
            pe.wait_ge(pad_weights, 32)
            nc.tensor.matmul(ps_w[:, 0, :], rel1[:, :], lin1[:, :], start=True, stop=True)
            nc.tensor.matmul(ps_w[:, 1, :], root1[:, :], lin1[:, :], start=True, stop=True)
            nc.tensor.matmul(ps_w[:, 2, :], rel2[:, :], lin2[:, :], start=True, stop=True)
            nc.tensor.matmul(ps_w[:, 3, :], root2[:, :], lin2[:, :], start=True, stop=True)
            nc.tensor.matmul(ps_f[:, 0, :], f1w1[:, :], f1w2[:, :], start=True, stop=True)
            nc.tensor.matmul(ps_f[:, 1, :], f2w1[:, :], f2w2[:, :], start=True, stop=True)
            nc.tensor.matmul(ps_b[:, 0:1], lin1[:, :], s["cols"][:, REL1B:REL1B + 1], start=True, stop=True)
            nc.tensor.matmul(ps_b[:, 1:2], lin2[:, :], s["cols"][:, REL2B:REL2B + 1],
                             start=True, stop=True).then_inc(products, 1)

        @block.vector
        def _(dve):
            dve.wait_ge(mask_loaded, 32)
            nc.vector.tensor_tensor(cont[:, :], dst_r[:, :], prv_r[:, :], ALU.is_equal).then_inc(masks, 1)
            dve.wait_ge(masks, 1)
            nc.vector.tensor_copy(cont16[:, :], cont[:, :]).then_inc(masks, 1)
            nc.vector.tensor_scalar(pen16[:, :], cont[:, :], -PENALTY, PENALTY, ALU.mult, ALU.add).then_inc(masks, 1)
            dve.wait_ge(idx_loaded, 64)
            nc.vector.tensor_tensor(same[:, :], dst[:, :], nxt[:, :], ALU.is_equal).then_inc(masks, 1)
            dve.wait_ge(masks, 4)
            nc.vector.scalar_tensor_tensor(s["scat"][:, :], same[:, :], float(SKIP), dst[:, :],
                                           ALU.mult, ALU.add).then_inc(masks, 1)
            dve.wait_ge(weights_loaded, 16 * len(loads))
            nc.vector.bn_stats(d_st[:, :], s["b3"][:, :]).then_inc(chain, 1)
            dve.wait_ge(chain, 1)
            nc.vector.bn_aggr(d_mv[:, :], d_st[:, :]).then_inc(chain, 1)
            dve.wait_ge(std_ready, 1)
            nc.vector.reciprocal(d_rs[:, :], d_sd[:, :]).then_inc(chain, 1)
            dve.wait_ge(chain, 3)
            nc.vector.tensor_scalar(row[:, :], s["b3"][:, :], d_mv[:, 0:1], d_rs[:, :],
                                    ALU.subtract, ALU.mult).then_inc(chain, 1)
            dve.wait_ge(chain, 4)
            nc.vector.tensor_tensor(row[:, :], row[:, :], s["g3"][:, :], ALU.mult).then_inc(chain, 1)
            dve.wait_ge(chain, 5)
            nc.vector.tensor_tensor(row[:, :], row[:, :], s["be3"][:, :], ALU.add).then_inc(chain, 1)
            dve.wait_ge(chain, 6)
            for j in range(G):
                nc.vector.tensor_scalar_max(s["default"][:, j, :], row[:, :], 0.0)
            dve.wait_ge(products, 1)
            for i, n in enumerate(("A1", "R1", "A2", "R2")):
                nc.vector.tensor_copy(s[n][:, :], ps_w[:, i, :])
            nc.vector.tensor_copy(s["FW1"][:, :], ps_f[:, 0, :])
            nc.vector.tensor_copy(s["FW2"][:, :], ps_f[:, 1, :])
            nc.vector.tensor_tensor(s["cols"][:, B1:B1 + 1], ps_b[:, 0:1], s["cols"][:, L1B:L1B + 1], ALU.add)
            nc.vector.tensor_tensor(s["cols"][:, B2:B2 + 1], ps_b[:, 1:2], s["cols"][:, L2B:L2B + 1], ALU.add)


def rows_of(table):
    return table.rearrange("(b p j) f -> b p (j f)", p=P, j=G)


def gather(nc, rows, table, idx, sem):
    for j in range(G):
        nc.gpsimd.indirect_dma_start(out=rows[:, j, :], out_offset=None, in_=table,
                                     in_offset=bass.IndirectOffsetOnAxis(ap=idx[:, j:j + 1], axis=0)).then_inc(sem, 16)


def scatter(nc, table, idx, rows, sem):
    for j in range(G):
        nc.gpsimd.indirect_dma_start(out=table, out_offset=bass.IndirectOffsetOnAxis(ap=idx[:, j:j + 1], axis=0),
                                     in_=rows[:, j, :], in_offset=None, bounds_check=table.shape[0] - 1,
                                     oob_is_err=False).then_inc(sem, 16)


def tile(j):
    return slice(j * P, (j + 1) * P)


def edges0(nc, a, tab, s, EB):
    with ExitStack() as ctx:
        def sb(name, shape, dt=F32):
            return ctx.enter_context(nc.sbuf_tensor(name, shape, dt))

        def ps(name):
            return [ctx.enter_context(nc.psum_tensor(f"{name}{i}", [P, G, P], F32)) for i in range(2)]

        sem = phase_semaphores(nc, ctx, "edges0")

        src_idx, dst_idx = sb("e0_src_idx", [P, 2, G], I32), sb("e0_dst_idx", [P, 2, G], I32)
        rows = sb("e0_rows", [P, 2, G, H])
        run = sb("e0_run", [P, 2, BLK])
        cont = sb("e0_cont", [1, 2, BLK], BF16)
        cnt = sb("e0_cnt", [1, 2, BLK])
        res = sb("e0_res", [P, 2, G, TW])
        ps_x, ps_r, ps_c = ps("e0_ps_x"), ps("e0_ps_r"), ps("e0_ps_c")
        gathered, scattered = [sem("gathered0"), sem("gathered1")], [sem("scattered0"), sem("scattered1")]
        cont_in = [sem("cont_in0"), sem("cont_in1")]
        idx_ready, dst_ready, turned, scanned, counted, back, stored, cleared, wide_zeroed = (
            sem(n) for n in ("idx_ready", "dst_ready", "turned", "scanned", "counted", "back", "stored", "cleared",
                             "wide_zeroed"))
        wide_flat = tab["wide"].rearrange("(c p r) f -> c p (r f)", c=EB, p=P)
        assert wide_flat.shape[2] <= 4096
        block = ctx.enter_context(nc.Block())

        @block.sync
        def _(sp):
            def step(t):
                if t.past(2):
                    sp.wait_ge(counted, t.b - 1)
                sp.dma_start(cont[:, t.slot, :], tab["cont"][:, bass.ds(t.b * BLK, BLK)]).then_inc(cont_in[t.slot], 16)
                half = wide_flat.shape[2]
                for c in range(0, half, 2048):
                    w = min(2048, half - c)
                    sp.dma_start(wide_flat[t.b][:, c:c + w], s["zero"][:, 0:w]).then_inc(wide_zeroed, 16)
            staggered(sp, EB, 2, 4, 0, step)
            sp.wait_ge(wide_zeroed, 16 * EB * -(-wide_flat.shape[2] // 2048))

        @block.gpsimd
        def _(pool):
            wait_values = WaitValues(pool, "edges0", 2)

            def step(t):
                if t.within(EB):
                    ready, freed = wait_values(t.b + 1, t.b - 1)
                    first_wait(pool, idx_ready)
                    pool.wait_ge(idx_ready, ready)
                    if t.past(2):
                        pool.wait_ge(turned, freed)
                    gather(nc, rows[:, t.slot], a["x"], src_idx[:, t.slot], gathered[t.slot])
                b = t.back(1)
                if b.within(EB):
                    ready, rows_ready = wait_values(b.b + 1, b.b + 1)
                    first_wait(pool, dst_ready)
                    pool.wait_ge(dst_ready, ready)
                    pool.wait_ge(stored, rows_ready)
                    scatter(nc, tab["narrow"], dst_idx[:, b.slot], res[:, b.slot], scattered[b.slot])
            nc.gpsimd.memset(res[:, :, :, :], 0.0).then_inc(cleared, 1)
            staggered(pool, EB, 2, 4, 1, step)
            for q in range(2):
                pool.wait_ge(scattered[q], 16 * G * EB // 2)

        @block.tensor
        def _(pe):
            def step(t):
                if t.within(EB):
                    pe.wait_ge(gathered[t.slot], t.q * (16 * G) + 16 * G)
                    if t.past(2):
                        pe.wait_ge(scanned, t.b - 1)
                    for j in range(G):
                        i = nc.tensor.transpose(ps_x[t.slot][:, j, :], rows[:, t.slot, j, :], s["ident"][:, :])
                    i.then_inc(turned, 1)
                b = t.back(1)
                if b.within(EB):
                    pe.wait_ge(scanned, b.b + 1)
                    pe.wait_ge(counted, b.b + 1)
                    if b.past(2):
                        pe.wait_ge(stored, b.b - 1)
                    for j in range(G):
                        nc.tensor.transpose(ps_r[b.slot][:, j, :], run[:, b.slot, tile(j)], s["ident"][:, :])
                    for j in range(G):
                        i = nc.tensor.matmul(ps_c[b.slot][:, 0, j:j + 1], cnt[:, b.slot, tile(j)], s["ones"][:, 0:1],
                                             start=True, stop=True)
                    i.then_inc(back, 1)
            staggered(pe, EB, 2, 4, 1, step)

        @block.vector
        def _(dve):
            def copy_idx(t):
                if t.past(2):
                    dve.wait_ge(gathered[t.slot], t.q * (16 * G))
                nc.vector.tensor_copy(src_idx[:, t.slot, :], s["src"][:, bass.ds(t.b * G, G)]).then_inc(idx_ready, 1)

            def step(t):
                if t.within(EB):
                    copy_idx(t)
                b = t.back(1)
                if b.within(EB):
                    if b.past(2):
                        dve.wait_ge(scattered[b.slot], b.q * (16 * G))
                    nc.vector.tensor_copy(dst_idx[:, b.slot, :],
                                          s["scat"][:, bass.ds(b.b * G, G)]).then_inc(dst_ready, 1)
                    if b.past(2):
                        dve.wait_ge(back, b.b - 1)
                    if b.past(1):
                        dve.wait_ge(counted, b.b)
                        dve.wait_ge(scanned, b.b)
                    dve.wait_ge(cont_in[b.slot], b.q * 16 + 16)
                    prev = 1 - b.slot
                    nc.vector.tensor_tensor_scan(cnt[:, b.slot, :], cont[:, b.slot, :], s["ones"][:, :],
                                                 initial=cnt[:, prev, BLK - 1:BLK] if b.past(1) else 0.0,
                                                 op0=ALU.mult, op1=ALU.add).then_inc(counted, 1)
                    dve.wait_ge(turned, b.b + 1)
                    nc.vector.tensor_tensor_scan(run[:, b.slot, :], s["mask"][:, bass.ds(b.b * BLK, BLK)],
                                                 ps_x[b.slot][:, :, :].rearrange("p j f -> p (j f)"),
                                                 initial=run[:, prev, BLK - 1:BLK] if b.past(1) else 0.0,
                                                 op0=ALU.add, op1=ALU.min).then_inc(scanned, 1)
            staggered(dve, EB, 2, 4, 1, step)

        @block.scalar
        def _(act):
            def step(t):
                act.wait_ge(back, t.b + 1)
                if t.past(2):
                    act.wait_ge(scattered[t.slot], t.q * (16 * G))
                nc.scalar.activation(res[:, t.slot, :, 0:H], ps_r[t.slot][:, :, :], ACT.Copy)
                nc.scalar.activation(res[:, t.slot, :, H], ps_c[t.slot][:, 0, 0:G], ACT.Copy).then_inc(stored, 1)
            act.wait_ge(cleared, 1)
            staggered(act, EB, 2, 4, 0, step)


def to4(row):
    return row[:, :].unsqueeze(1).broadcast_to([P, G, H])


def per_node(v):
    return v.unsqueeze(2).broadcast_to([P, G, H])


class Norm:

    def __init__(self, nc, ctx, sem, name="ln"):
        def sb(n, shape):
            return ctx.enter_context(nc.sbuf_tensor(f"{name}_{n}", shape, F32))

        self.st, self.mv = sb("st", [P, 2, G, 6]), sb("mv", [P, 2, G, 2])
        self.sd, self.rs, self.nm = sb("sd", [P, 2, G]), sb("rs", [P, 2, G]), sb("nm", [P, 2, G])
        self.stats_done, self.moments, self.std, self.inv, self.scale_ready, self.applied = (
            sem(f"{name}_{n}") for n in ("stats", "moments", "std", "inv", "scale", "applied"))


def norm_stats(nc, dve, ln, b, k, v):
    done = dve.snap(b + 1) if not isinstance(b, int) else b + 1
    for j in range(G):
        i = nc.vector.bn_stats(ln.st[:, k, j, :], v[:, j, :])
    i.then_inc(ln.stats_done, 1)
    first_wait(dve, ln.stats_done)
    dve.wait_ge(ln.stats_done, done)
    for j in range(G):
        i = nc.vector.bn_aggr(ln.mv[:, k, j, :], ln.st[:, k, j, :])
    i.then_inc(ln.moments, 1)


def norm_std(nc, act, ln, b, k, eps):
    act.wait_ge(ln.moments, b + 1)
    nc.scalar.activation(ln.sd[:, k, :], ln.mv[:, k, :, 1], ACT.Sqrt, bias=eps).then_inc(ln.std, 1)


def norm_scale(nc, dve, ln, b, k, times=None):
    dve.wait_ge(ln.std, b + 1)
    nc.vector.reciprocal(ln.rs[:, k, :], ln.sd[:, k, :]).then_inc(ln.inv, 1)
    n = 1
    if times is not None:
        dve.wait_ge(ln.inv, b * 2 + 1)
        nc.vector.tensor_tensor(ln.rs[:, k, :], ln.rs[:, k, :], times, ALU.mult).then_inc(ln.inv, 1)
        n = 2
    dve.wait_ge(ln.inv, b * n + n)
    nc.vector.scalar_tensor_tensor(ln.nm[:, k, :], ln.mv[:, k, :, 0], -1.0, ln.rs[:, k, :],
                                   ALU.mult, ALU.mult).then_inc(ln.scale_ready, 1)


def norm_apply(nc, act, ln, b, k, dst, v):
    act.wait_ge(ln.scale_ready, b + 1)
    for j in range(G):
        i = nc.scalar.activation(dst[:, j, :], v[:, j, :], ACT.Identity, bias=ln.nm[:, k, j:j + 1],
                                 scale=ln.rs[:, k, j:j + 1])
    i.then_inc(ln.applied, 1)


def nodes0(nc, a, tab, s, NB):
    with ExitStack() as ctx:
        def sb(name, shape, dt=F32):
            return ctx.enter_context(nc.sbuf_tensor(name, shape, dt))

        def ps(name):
            return [ctx.enter_context(nc.psum_tensor(f"{name}{i}", [P, G, P], F32)) for i in range(2)]

        sem = phase_semaphores(nc, ctx, "nodes0")

        x = sb("n0_x", [P, 4, G, H])
        t0 = sb("n0_t", [P, 2, G, TW])
        has = sb("n0_has", [P, 2, G])
        md = sb("n0_md", [P, 2, G, H])
        xT, mdT = sb("n0_xT", [P, 2, BLK]), sb("n0_mdT", [P, 2, BLK])
        v = sb("n0_v", [P, 2, G, H])
        o = sb("n0_o", [P, 2, G, H])
        ps_x, ps_m, ps_o = ps("n0_ps_x"), ps("n0_ps_m"), ps("n0_ps_o")
        ln = Norm(nc, ctx, sem)
        x_in, t_in = [sem(f"x_in{i}") for i in range(4)], [sem(f"t_in{i}") for i in range(2)]
        saved = [sem(f"saved{i}") for i in range(2)]
        mask_in, has_ready, masked, md_ready, x_turned, md_turned, x_copied, md_copied, product, biased, summed = (
            sem(n) for n in ("mask_in", "has_ready", "masked", "md_ready", "x_turned", "md_turned", "x_copied",
                             "md_copied", "product", "biased", "summed"))
        x_v, t_v, o_v = rows_of(a["x"]), rows_of(tab["narrow"]), rows_of(tab["x1"])
        block = ctx.enter_context(nc.Block())

        @block.sync
        def _(sp):
            def step(t):
                if t.within(NB):
                    if t.past(4):
                        sp.wait_ge(summed, t.b - 3)
                    sp.dma_start(x[:, t.slot], x_v[t.b]).then_inc(x_in[t.slot], 16)
                    if t.past(2):
                        sp.wait_ge(md_ready, t.b - 1)
                    sp.dma_start(t0[:, t.slot % 2], t_v[t.b]).then_inc(t_in[t.slot % 2], 16)
                b = t.back(4)
                if b.within(NB):
                    sp.wait_ge(ln.applied, b.b + 1)
                    sp.dma_start(o_v[b.b], o[:, b.slot % 2]).then_inc(saved[b.slot % 2], 16)
            sp.dma_start(s["mask"][:, :], tab["cont"].broadcast_to([P, s["mask"].shape[1]]),
                         max_dma_last_dim=16384).then_inc(mask_in, 16)
            staggered(sp, NB, 4, 8, 4, step)
            for q in range(2):
                sp.wait_ge(saved[q], 16 * NB // 2)
            sp.wait_ge(mask_in, 16)

        @block.vector
        def _(dve):
            def step(t):
                b = t.back(3)
                if b.within(NB):
                    norm_scale(nc, dve, ln, b.b, b.slot % 2)
                if t.within(NB):
                    k = t.slot % 2
                    dve.wait_ge(t_in[k], t.q * 32 + (t.slot // 2) * 16 + 16)
                    if t.past(2):
                        dve.wait_ge(masked, t.b - 1)
                    nc.vector.tensor_scalar_min(has[:, k, :], t0[:, k, :, H], 1.0).then_inc(has_ready, 1)
                    nc.vector.tensor_scalar_add(s["deg"][:, bass.ds(t.b * G, G)], t0[:, k, :, H],
                                                1.0).then_inc(has_ready, 1)
                b = t.back(2)
                if b.within(NB):
                    k = b.slot % 2
                    dve.wait_ge(product, b.b + 1)
                    if b.past(2):
                        dve.wait_ge(ln.applied, b.b - 1)
                    nc.vector.tensor_tensor(v[:, k], ps_o[k][:, :, :], to4(s["b0"]), ALU.add).then_inc(biased, 1)
                    dve.wait_ge(biased, b.b + 1)
                    nc.vector.scalar_tensor_tensor(v[:, k], v[:, k], 0.0, x[:, b.slot],
                                                   ALU.max, ALU.add).then_inc(summed, 1)
                    dve.wait_ge(summed, b.b + 1)
                    norm_stats(nc, dve, ln, b.b, k, v[:, k])
            staggered(dve, NB, 4, 8, 3, step)

        @block.gpsimd
        def _(pool):
            def step(t):
                k = t.slot % 2
                pool.wait_ge(x_in[t.slot], t.q * 16 + 16)
                pool.wait_ge(has_ready, t.b * 2 + 2)
                if t.past(2):
                    pool.wait_ge(md_turned, t.b - 1)
                nc.gpsimd.tensor_tensor(md[:, k], x[:, t.slot], per_node(has[:, k, :]), ALU.mult).then_inc(masked, 1)
                pool.wait_ge(masked, t.b + 1)
                nc.gpsimd.tensor_tensor(md[:, k], md[:, k], t0[:, k, :, 0:H], ALU.subtract).then_inc(md_ready, 1)
            staggered(pool, NB, 4, 8, 0, step)

        @block.tensor
        def _(pe):
            def step(t):
                if t.within(NB):
                    k = t.slot % 2
                    pe.wait_ge(x_in[t.slot], t.q * 16 + 16)
                    if t.past(2):
                        pe.wait_ge(x_copied, t.b - 1)
                    for j in range(G):
                        i = nc.tensor.transpose(ps_x[k][:, j, :], x[:, t.slot, j, :], s["ident"][:, :])
                    i.then_inc(x_turned, 1)
                b = t.back(1)
                if b.within(NB):
                    k = b.slot % 2
                    pe.wait_ge(md_ready, b.b + 1)
                    if b.past(2):
                        pe.wait_ge(md_copied, b.b - 1)
                    for j in range(G):
                        i = nc.tensor.transpose(ps_m[k][:, j, :], md[:, k, j, :], s["ident"][:, :])
                    i.then_inc(md_turned, 1)
                b = t.back(2)
                if b.within(NB):
                    k = b.slot % 2
                    pe.wait_ge(x_copied, b.b + 1)
                    pe.wait_ge(md_copied, b.b + 1)
                    if b.past(2):
                        pe.wait_ge(biased, b.b - 1)
                    for j in range(G):
                        nc.tensor.matmul(ps_o[k][:, j, :], xT[:, k, tile(j)], s["w0"][:, 0, :], start=True, stop=False)
                        i = nc.tensor.matmul(ps_o[k][:, j, :], mdT[:, k, tile(j)], s["w0"][:, 1, :],
                                             start=False, stop=True)
                    i.then_inc(product, 1)
            staggered(pe, NB, 4, 8, 2, step)

        @block.scalar
        def _(act):
            def step(t):
                if t.within(NB):
                    k = t.slot % 2
                    act.wait_ge(x_turned, t.b + 1)
                    if t.past(2):
                        act.wait_ge(product, t.b - 1)
                    nc.scalar.activation(xT[:, k, :], ps_x[k][:, :, :].rearrange("p j f -> p (j f)"),
                                         ACT.Copy).then_inc(x_copied, 1)
                b = t.back(1)
                if b.within(NB):
                    k = b.slot % 2
                    act.wait_ge(md_turned, b.b + 1)
                    if b.past(2):
                        act.wait_ge(product, b.b - 1)
                    nc.scalar.activation(mdT[:, k, :], ps_m[k][:, :, :].rearrange("p j f -> p (j f)"),
                                         ACT.Copy).then_inc(md_copied, 1)
                b = t.back(3)
                if b.within(NB):
                    k = b.slot % 2
                    if b.past(2):
                        act.wait_ge(saved[k], b.q * 32 + (b.slot // 2) * 16)
                    norm_apply(nc, act, ln, b.b, k, o[:, k], v[:, k])
                b = t.back(2)
                if b.within(NB):
                    norm_std(nc, act, ln, b.b, b.slot % 2, s["eps"][:, 0:1])
            staggered(act, NB, 4, 8, 3, step)


def edges1(nc, a, tab, s, EB):
    with ExitStack() as ctx:
        def sb(name, shape, dt=F32):
            return ctx.enter_context(nc.sbuf_tensor(name, shape, dt))

        def ps(name):
            return ctx.enter_context(nc.psum_tensor(name, [P, G, P], F32))

        sem = phase_semaphores(nc, ctx, "edges1")

        src_idx, dst_idx = sb("e1_src_idx", [P, 2, G], I32), sb("e1_dst_idx", [P, 2, G], I32)
        rows = sb("e1_rows", [P, 2, G, H])
        ea = sb("e1_ea", [FA, 2, BLK])
        xT, xs = sb("e1_xT", [P, 2, BLK]), sb("e1_xs", [P, 2, BLK])
        m1, m2 = sb("e1_m1", [P, BLK]), sb("e1_m2", [P, BLK])
        run1, run2 = sb("e1_run1", [P, 2, BLK]), sb("e1_run2", [P, 2, BLK])
        res = sb("e1_res", [P, 2, G, 2 * H])
        ps_x, ps_l, ps_f1, ps_f2, ps_o1, ps_o2 = (ps(f"e1_ps{i}") for i in range(6))
        gathered, scattered = [sem("gathered0"), sem("gathered1")], [sem("scattered0"), sem("scattered1")]
        ea_in = [sem("ea_in0"), sem("ea_in1")]
        idx_ready, dst_ready, turned, copied, lined, active, f_ready, mul1, mul2, scanned1, scanned2, product, stored = (
            sem(n) for n in ("idx_ready", "dst_ready", "turned", "copied", "lined", "active", "f_ready", "mul1", "mul2",
                             "scanned1", "scanned2", "product", "stored"))

        def flat(bank):
            return bank[:, :, :].rearrange("p j f -> p (j f)")
        block = ctx.enter_context(nc.Block())

        @block.sync
        def _(sp):
            def step(t):
                if t.past(2):
                    sp.wait_ge(f_ready, t.b - 1)
                sp.dma_start(ea[:, t.slot, :], a["edge_attr_T"][:, bass.ds(t.b * BLK, BLK)]).then_inc(ea_in[t.slot], 16)
            staggered(sp, EB, 2, 4, 0, step)

        @block.gpsimd
        def _(pool):
            wait_values = WaitValues(pool, "edges1", 2)

            def step(t):
                if t.within(EB):
                    ready, freed = wait_values(t.b + 1, t.b - 1)
                    first_wait(pool, idx_ready)
                    pool.wait_ge(idx_ready, ready)
                    if t.past(2):
                        pool.wait_ge(turned, freed)
                    gather(nc, rows[:, t.slot], tab["x1"], src_idx[:, t.slot], gathered[t.slot])
                b = t.back(2)
                if b.within(EB):
                    ready, rows_ready = wait_values(b.b + 1, b.b * 2 + 2)
                    first_wait(pool, dst_ready)
                    pool.wait_ge(dst_ready, ready)
                    pool.wait_ge(stored, rows_ready)
                    scatter(nc, tab["wide"], dst_idx[:, b.slot], res[:, b.slot], scattered[b.slot])
            staggered(pool, EB, 2, 4, 2, step)
            for q in range(2):
                pool.wait_ge(scattered[q], 16 * G * EB // 2)

        @block.tensor
        def _(pe):
            def step(t):
                if t.within(EB):
                    pe.wait_ge(gathered[t.slot], t.q * (16 * G) + 16 * G)
                    if t.past(1):
                        pe.wait_ge(copied, t.b)
                    for j in range(G):
                        i = nc.tensor.transpose(ps_x[:, j, :], rows[:, t.slot, j, :], s["ident"][:, :])
                    i.then_inc(turned, 1)
                    pe.wait_ge(ea_in[t.slot], t.q * 16 + 16)
                    if t.past(1):
                        pe.wait_ge(mul2, t.b)
                    nc.tensor.matmul(flat(ps_f1), s["FW1"][:, :], ea[:, t.slot, :], start=True, stop=True)
                    nc.tensor.matmul(flat(ps_f2), s["FW2"][:, :], ea[:, t.slot, :],
                                     start=True, stop=True).then_inc(f_ready, 1)
                    pe.wait_ge(copied, t.b + 1)
                    if t.past(1):
                        pe.wait_ge(active, t.b)
                    nc.tensor.matmul(flat(ps_l), s["lin"][:, :], xT[:, t.slot, :], start=True, stop=True).then_inc(lined, 1)
                b = t.back(1)
                if b.within(EB):
                    pe.wait_ge(scanned1, b.b + 1)
                    pe.wait_ge(scanned2, b.b + 1)
                    if b.past(1):
                        pe.wait_ge(stored, b.b * 2)
                    for j in range(G):
                        nc.tensor.matmul(ps_o1[:, j, :], run1[:, b.slot, tile(j)], s["A1"][:, :], start=True, stop=True)
                    for j in range(G):
                        i = nc.tensor.matmul(ps_o2[:, j, :], run2[:, b.slot, tile(j)], s["A2"][:, :],
                                             start=True, stop=True)
                    i.then_inc(product, 1)
            staggered(pe, EB, 2, 4, 1, step)

        @block.scalar
        def _(act):
            def step(t):
                if t.within(EB):
                    act.wait_ge(turned, t.b + 1)
                    if t.past(2):
                        act.wait_ge(lined, t.b - 1)
                    nc.scalar.activation(xT[:, t.slot, :], flat(ps_x), ACT.Copy).then_inc(copied, 1)
                    act.wait_ge(lined, t.b + 1)
                    if t.past(2):
                        act.wait_ge(mul2, t.b - 1)
                    nc.scalar.activation(xs[:, t.slot, :], flat(ps_l), ACT.Silu,
                                         bias=s["cols"][:, LIN_B:LIN_B + 1]).then_inc(active, 1)
                b = t.back(1)
                if b.within(EB):
                    act.wait_ge(product, b.b + 1)
                    if b.past(2):
                        act.wait_ge(scattered[b.slot], b.q * (16 * G))
                    nc.scalar.activation(res[:, b.slot, :, 0:H], ps_o1[:, :, :], ACT.Copy).then_inc(stored, 1)
                    nc.scalar.activation(res[:, b.slot, :, H:2 * H], ps_o2[:, :, :], ACT.Copy).then_inc(stored, 1)
            staggered(act, EB, 2, 4, 1, step)

        @block.vector
        def _(dve):
            def step(t):
                if t.within(EB):
                    if t.past(2):
                        dve.wait_ge(gathered[t.slot], t.q * (16 * G))
                    nc.vector.tensor_copy(src_idx[:, t.slot, :], s["src"][:, bass.ds(t.b * G, G)]).then_inc(idx_ready, 1)
                b = t.back(1)
                if b.within(EB):
                    prev = 1 - b.slot
                    dve.wait_ge(f_ready, b.b + 1)
                    dve.wait_ge(active, b.b + 1)
                    if b.past(1):
                        dve.wait_ge(scanned1, b.b)
                        dve.wait_ge(scanned2, b.b)
                    nc.vector.tensor_tensor(m1[:, :], flat(ps_f1), xs[:, b.slot, :], ALU.mult).then_inc(mul1, 1)
                    nc.vector.tensor_tensor(m2[:, :], flat(ps_f2), xs[:, b.slot, :], ALU.mult).then_inc(mul2, 1)
                    if b.past(2):
                        dve.wait_ge(product, b.b - 1)
                    for m, run, ready, done in ((m1, run1, mul1, scanned1), (m2, run2, mul2, scanned2)):
                        dve.wait_ge(ready, b.b + 1)
                        nc.vector.tensor_tensor_scan(run[:, b.slot, :], s["mask"][:, bass.ds(b.b * BLK, BLK)], m[:, :],
                                                     initial=run[:, prev, BLK - 1:BLK] if b.past(1) else 0.0,
                                                     op0=ALU.mult, op1=ALU.add).then_inc(done, 1)
                    if b.past(2):
                        dve.wait_ge(scattered[b.slot], b.q * (16 * G))
                    nc.vector.tensor_copy(dst_idx[:, b.slot, :],
                                          s["scat"][:, bass.ds(b.b * G, G)]).then_inc(dst_ready, 1)
            staggered(dve, EB, 2, 4, 1, step)


def nodes1(nc, tab, s, NB, LAST):
    with ExitStack() as ctx:
        def sb(name, shape, dt=F32):
            return ctx.enter_context(nc.sbuf_tensor(name, shape, dt))

        def ps(name):
            return ctx.enter_context(nc.psum_tensor(name, [P, G, P], F32))

        sem = phase_semaphores(nc, ctx, "nodes1")

        def flat(bank):
            return bank[:, :, :].rearrange("p j f -> p (j f)")

        def col(c):
            return s["cols"][:, c:c + 1]

        x, w = sb("n1_x", [P, 2, G, H]), sb("n1_w", [P, 2, G, 2 * H])
        xT, xx = sb("n1_xT", [P, 2, BLK]), sb("n1_xx", [P, 4, BLK])
        g1, g2 = sb("n1_g1", [P, 2, BLK]), sb("n1_g2", [P, 2, BLK])
        h1, h2 = sb("n1_h1", [P, 2, BLK]), sb("n1_h2", [P, 2, BLK])
        hs = [sb(f"n1_r{i}", [P, 2, BLK]) for i in range(4)]
        act_out = [sb(f"n1_s{i}", [P, BLK]) for i in range(3)]
        ps_x, ps_t, ps_l, ps_u1, ps_u2, ps_h, ps_ra, ps_rb = (ps(f"n1_ps{i}") for i in range(8))
        ps_r = (ps_ra, ps_rb, ps_ra)
        x_in, w_in, saved = ([sem(f"{n}{i}") for i in range(2)] for n in ("x_in", "w_in", "saved"))
        filled = sem("filled")
        (x_turned, x_copied, t1_turned, t2_turned, t1_copied, t2_copied, lined, active, u_done1, u_done2, pre1, pre2,
         h_ready1, h_ready2, cat_done, r0_ready, counted) = (sem(n) for n in (
             "x_turned", "x_copied", "t1_turned", "t2_turned", "t1_copied", "t2_copied", "lined", "active", "u_done1",
             "u_done2", "pre1", "pre2", "h_ready1", "h_ready2", "cat_done", "r0_ready", "counted"))
        r_done, r_act, r_added = ([sem(f"{n}{i}") for i in range(3)] for n in ("r_done", "r_act", "r_added"))
        x_v, w_v, d_v = rows_of(tab["x1"]), rows_of(tab["wide"]), rows_of(tab["last"])
        block = ctx.enter_context(nc.Block())

        @block.sync
        def _(sp):
            def step(t):
                if t.within(NB):
                    k = t.slot % 2
                    if t.past(2):
                        sp.wait_ge(x_turned, t.b - 1)
                    sp.dma_start(x[:, k], x_v[t.b]).then_inc(x_in[k], 16)
                    if t.past(2):
                        sp.wait_ge(t2_turned, t.b - 1)
                    sp.dma_start(w[:, k], w_v[t.b]).then_inc(w_in[k], 16)
                    sp.dma_start(d_v[t.b], s["default"][:, :, :]).then_inc(filled, 16)
                b = t.back(7)
                if b.within(NB):
                    sp.wait_ge(r_added[2], b.b + 1)
                    sp.dma_start(tab["hT"][b.b], hs[3][:, b.slot % 2, :]).then_inc(saved[b.slot % 2], 16)
            staggered(sp, NB, 4, 12, 7, step)
            for q in range(2):
                sp.wait_ge(saved[q], 16 * NB // 2)
            sp.wait_ge(filled, 16 * NB)

        @block.tensor
        def _(pe):
            def residual(i, b):
                if b.within(NB):
                    if i == 0:
                        pe.wait_ge(r0_ready, b.b + 1)
                    else:
                        pe.wait_ge(r_added[i - 1], b.b + 1)
                    if i == 1 and b.past(1):
                        pe.wait_ge(r_act[1], b.b)
                    if i == 0 and b.past(3):
                        pe.wait_ge(r_act[2], b.b - 2)
                    if i == 2:
                        pe.wait_ge(r_act[0], (b.b + 3) if not isinstance(b.q, int) else min(b.b + 3, NB))
                        if isinstance(b.q, int) and b.past(1):
                            pe.wait_ge(r_act[2], b.b)
                    nc.tensor.matmul(flat(ps_r[i]), s["lins"][:, i, :], hs[i][:, b.slot % 2, :],
                                     start=True, stop=True).then_inc(r_done[i], 1)

            def step(t):
                residual(0, t.back(4))
                d = t.back(1)
                if d.within(NB):
                    kd = d.slot % 2
                    pe.wait_ge(w_in[kd], d.q * 32 + (d.slot // 2) * 16 + 16)
                    if d.past(1):
                        pe.wait_ge(t2_copied, d.b)
                    for j in range(G):
                        i = nc.tensor.transpose(ps_t[:, j, :], w[:, kd, j, 0:H], s["ident"][:, :])
                    i.then_inc(t1_turned, 1)
                c = t.back(2)
                if c.within(NB):
                    pe.wait_ge(active, c.b + 1)
                    if c.past(1):
                        pe.wait_ge(pre1, c.b)
                    nc.tensor.matmul(flat(ps_u1), s["R1"][:, :], xx[:, c.slot, :],
                                     start=True, stop=True).then_inc(u_done1, 1)
                residual(1, t.back(5))
                if t.within(NB):
                    k = t.slot % 2
                    pe.wait_ge(x_in[k], t.q * 32 + (t.slot // 2) * 16 + 16)
                    if t.past(1):
                        pe.wait_ge(x_copied, t.b)
                    for j in range(G):
                        i = nc.tensor.transpose(ps_x[:, j, :], x[:, k, j, :], s["ident"][:, :])
                    i.then_inc(x_turned, 1)
                if d.within(NB):
                    pe.wait_ge(t1_copied, d.b + 1)
                    for j in range(G):
                        i = nc.tensor.transpose(ps_t[:, j, :], w[:, kd, j, H:2 * H], s["ident"][:, :])
                    i.then_inc(t2_turned, 1)
                if c.within(NB):
                    if c.past(1):
                        pe.wait_ge(pre2, c.b)
                    nc.tensor.matmul(flat(ps_u2), s["R2"][:, :], xx[:, c.slot, :],
                                     start=True, stop=True).then_inc(u_done2, 1)
                residual(2, t.back(6))
                b = t.back(1)
                if b.within(NB):
                    pe.wait_ge(x_copied, b.b + 1)
                    if b.past(1):
                        pe.wait_ge(active, b.b)
                    nc.tensor.matmul(flat(ps_l), s["lin"][:, :], xT[:, b.slot % 2, :],
                                     start=True, stop=True).then_inc(lined, 1)
                b = t.back(3)
                if b.within(NB):
                    pe.wait_ge(h_ready1, b.b + 1)
                    pe.wait_ge(h_ready2, b.b + 1)
                    if b.past(1):
                        pe.wait_ge(r0_ready, b.b)
                    nc.tensor.matmul(flat(ps_h), s["cat"][:, 0, :], h1[:, b.slot % 2, :], start=True, stop=False)
                    nc.tensor.matmul(flat(ps_h), s["cat"][:, 1, :], h2[:, b.slot % 2, :],
                                     start=False, stop=True).then_inc(cat_done, 1)
            staggered(pe, NB, 4, 12, 6, step)

        @block.scalar
        def _(act):
            def residual(i, b):
                if b.within(NB):
                    act.wait_ge(r_done[i], b.b + 1)
                    if b.past(1):
                        act.wait_ge(r_added[i], b.b)
                    nc.scalar.activation(act_out[i][:, :], flat(ps_r[i]), ACT.Silu, bias=col(LS0 + i)).then_inc(r_act[i], 1)

            def step(t):
                k = t.slot % 2
                residual(0, t.back(4))
                d = t.back(1)
                if d.within(NB):
                    act.wait_ge(t1_turned, d.b + 1)
                    if d.past(2):
                        act.wait_ge(h_ready1, d.b - 1)
                    nc.scalar.activation(g1[:, d.slot % 2, :], flat(ps_t), ACT.Copy).then_inc(t1_copied, 1)
                residual(1, t.back(5))
                if t.within(NB):
                    act.wait_ge(x_turned, t.b + 1)
                    if t.past(2):
                        act.wait_ge(lined, t.b - 1)
                    nc.scalar.activation(xT[:, k, :], flat(ps_x), ACT.Copy).then_inc(x_copied, 1)
                c = t.back(2)
                if c.within(NB):
                    act.wait_ge(pre1, c.b + 1)
                    if c.past(2):
                        act.wait_ge(cat_done, c.b - 1)
                    nc.scalar.activation(h1[:, c.slot % 2, :], g1[:, c.slot % 2, :], ACT.Silu,
                                         bias=col(B1)).then_inc(h_ready1, 1)
                if d.within(NB):
                    act.wait_ge(t2_turned, d.b + 1)
                    if d.past(2):
                        act.wait_ge(h_ready2, d.b - 1)
                    nc.scalar.activation(g2[:, d.slot % 2, :], flat(ps_t), ACT.Copy).then_inc(t2_copied, 1)
                if c.within(NB):
                    act.wait_ge(pre2, c.b + 1)
                    nc.scalar.activation(h2[:, c.slot % 2, :], g2[:, c.slot % 2, :], ACT.Silu,
                                         bias=col(B2)).then_inc(h_ready2, 1)
                residual(2, t.back(6))
                b = t.back(1)
                if b.within(NB):
                    act.wait_ge(lined, b.b + 1)
                    if b.past(4):
                        act.wait_ge(r0_ready, b.b - 3)
                    nc.scalar.activation(xx[:, b.slot, :], flat(ps_l), ACT.Silu, bias=col(LIN_B)).then_inc(active, 1)
            staggered(act, NB, 4, 12, 6, step)

        @block.vector
        def _(dve):
            def step(t):
                b = t.back(4)
                if b.within(NB):
                    dve.wait_ge(r_act[0], b.b + 1)
                    if b.past(2):
                        dve.wait_ge(r_done[1], b.b - 1)
                        dve.wait_ge(r_added[1], b.b - 1)
                    nc.vector.tensor_tensor(hs[1][:, b.slot % 2, :], act_out[0][:, :], hs[0][:, b.slot % 2, :],
                                            ALU.add).then_inc(r_added[0], 1)
                c = t.back(2)
                if c.within(NB):
                    k = c.slot % 2
                    dve.wait_ge(u_done1, c.b + 1)
                    dve.wait_ge(t1_copied, c.b + 1)
                    nc.vector.tensor_tensor(g1[:, k, :], flat(ps_u1), g1[:, k, :], ALU.add).then_inc(pre1, 1)
                    dve.wait_ge(u_done2, c.b + 1)
                    dve.wait_ge(t2_copied, c.b + 1)
                    nc.vector.tensor_tensor(g2[:, k, :], flat(ps_u2), g2[:, k, :], ALU.add).then_inc(pre2, 1)
                b = t.back(3)
                if b.within(NB):
                    dve.wait_ge(cat_done, b.b + 1)
                    if b.past(2):
                        dve.wait_ge(r_added[0], b.b - 1)
                        dve.wait_ge(r_done[0], b.b - 1)
                    nc.vector.scalar_tensor_tensor(hs[0][:, b.slot % 2, :], flat(ps_h), col(CAT_B),
                                                   xx[:, b.slot, :], ALU.add, ALU.add).then_inc(r0_ready, 1)
                b = t.back(7)
                if b.within(NB):
                    dve.wait_ge(r_added[2], b.b + 1)
                    last = isinstance(b.q, int) and b.b == NB - 1
                    v = hs[3][:, b.slot % 2, :]
                    if last:
                        v = v.rearrange("f (j p) -> f j p", j=G)[:, :, 0:LAST // G]
                    nc.vector.bn_stats(s["stats"][:, b.b, :], v).then_inc(counted, 1)
            staggered(dve, NB, 4, 12, 7, step)

        @block.gpsimd
        def _(pool):
            def residual(i, b):
                if b.within(NB):
                    k = b.slot % 2
                    pool.wait_ge(r_act[i], b.b + 1)
                    if b.past(2):
                        if i == 2:
                            pool.wait_ge(saved[k], b.q * 32 + (b.slot // 2) * 16)
                            pool.wait_ge(counted, b.b - 1)
                        else:
                            pool.wait_ge(r_done[i + 1], b.b - 1)
                            pool.wait_ge(r_added[i + 1], b.b - 1)
                    nc.gpsimd.tensor_tensor(hs[i + 1][:, k, :], act_out[i][:, :], hs[i][:, k, :],
                                            ALU.add).then_inc(r_added[i], 1)

            def step(t):
                residual(1, t.back(5))
                residual(2, t.back(6))
            staggered(pool, NB, 4, 12, 6, step)


def norm1(nc, tab, s, NB):
    with ExitStack() as ctx:
        def sb(name, shape, dt=F32):
            return ctx.enter_context(nc.sbuf_tensor(name, shape, dt))

        def ps(name):
            return [ctx.enter_context(nc.psum_tensor(f"{name}{i}", [P, G, P], F32)) for i in range(2)]

        sem = phase_semaphores(nc, ctx, "norm1")

        def col(c):
            return s["cols"][:, c:c + 1]

        small = sb("nm_small", [P, 16])
        shift = sb("nm_shift", [P, P])
        wn, row = sb("nm_w", [P, H]), sb("nm_row", [P, H])
        x, h = sb("nm_x", [P, 4, G, H]), sb("nm_h", [P, 2, BLK])
        v, o, xc = sb("nm_v", [P, 2, G, H]), sb("nm_o", [P, 2, G, H]), sb("nm_xc", [P, 2, G, H])
        ps_o = ps("nm_ps_o")
        ps_row = ctx.enter_context(nc.psum_tensor("nm_ps_row", [P, H], F32))
        ln = Norm(nc, ctx, sem, "nm_ln")
        x_in, h_in = [sem(f"x_in{i}") for i in range(4)], [sem(f"h_in{i}") for i in range(2)]
        saved = [sem(f"saved{i}") for i in range(2)]
        chain, var_ready, roots, shift_ready, row_product, weights, product, xc_ready, summed = (
            sem(n) for n in ("chain", "var_ready", "roots", "shift_ready", "row_product", "weights", "product",
                             "xc_ready", "summed"))
        x_v, o_v = rows_of(tab["x1"]), rows_of(tab["y2"])
        block = ctx.enter_context(nc.Block())
        MEAN, VAR, K, K2, V2, SD, SC, MSM, TV = range(9)

        def c1(i):
            return small[:, i:i + 1]

        @block.sync
        def _(sp):
            def step(t):
                if t.within(NB):
                    k = t.slot % 2
                    if t.past(4):
                        sp.wait_ge(xc_ready, t.b - 3)
                    sp.dma_start(x[:, t.slot], x_v[t.b]).then_inc(x_in[t.slot], 16)
                    if t.past(2):
                        sp.wait_ge(product, t.b - 1)
                    sp.dma_start(h[:, k], tab["hT"][t.b]).then_inc(h_in[k], 16)
                b = t.back(3)
                if b.within(NB):
                    sp.wait_ge(ln.applied, b.b + 1)
                    sp.dma_start(o_v[b.b], o[:, b.slot % 2]).then_inc(saved[b.slot % 2], 16)
            staggered(sp, NB, 4, 8, 3, step)
            for q in range(2):
                sp.wait_ge(saved[q], 16 * NB // 2)

        @block.gpsimd
        def _(pool):
            def step(t):
                k = t.slot % 2
                pool.wait_ge(x_in[t.slot], t.q * 16 + 16)
                if t.past(2):
                    pool.wait_ge(summed, t.b - 1)
                nc.gpsimd.tensor_tensor(xc[:, k], x[:, t.slot], to4(row), ALU.add).then_inc(xc_ready, 1)
            pool.wait_ge(weights, 2)
            staggered(pool, NB, 4, 8, 0, step)

        @block.tensor
        def _(pe):
            pe.wait_ge(shift_ready, 1)
            nc.tensor.matmul(ps_row[:, :], shift[:, :], s["fin"][:, :], start=True, stop=True).then_inc(row_product, 1)
            pe.wait_ge(weights, 1)

            def step(t):
                k = t.slot % 2
                pe.wait_ge(h_in[k], t.q * 32 + (t.slot // 2) * 16 + 16)
                if t.past(2):
                    pe.wait_ge(summed, t.b - 1)
                for j in range(G):
                    i = nc.tensor.matmul(ps_o[k][:, j, :], h[:, k, tile(j)], wn[:, :], start=True, stop=True)
                i.then_inc(product, 1)
            staggered(pe, NB, 4, 8, 0, step)

        @block.vector
        def _(dve):
            n = [0]

            def then(i):
                n[0] += 1
                i.then_inc(chain, 1)
                dve.wait_ge(chain, n[0])
            then(nc.vector.bn_aggr(small[:, MEAN:VAR + 1], s["stats"][:, :, :].rearrange("p b c -> p (b c)")))
            then(nc.vector.tensor_scalar(c1(K), col(NORM_MS), -1.0, 1.0, ALU.mult, ALU.add))
            then(nc.vector.tensor_tensor(c1(K), c1(K), c1(MEAN), ALU.mult))
            then(nc.vector.tensor_tensor(c1(K2), c1(K), c1(K), ALU.mult))
            nc.vector.tensor_tensor(c1(V2), c1(VAR), c1(K2), ALU.add).then_inc(var_ready, 1)
            dve.wait_ge(roots, 2)
            then(nc.vector.reciprocal(s["dis"][:, :], s["sdeg"][:, :]))
            then(nc.vector.reciprocal(c1(SC), c1(SD)))
            then(nc.vector.tensor_tensor(c1(SC), c1(SC), col(NORM_W), ALU.mult))
            nc.vector.tensor_scalar(wn[:, :], s["fin"][:, :], c1(SC), None, ALU.mult).then_inc(weights, 1)
            then(nc.vector.tensor_tensor(c1(MSM), c1(MEAN), col(NORM_MS), ALU.mult))
            then(nc.vector.tensor_tensor(c1(MSM), c1(MSM), c1(SC), ALU.mult))
            then(nc.vector.tensor_tensor(c1(TV), col(NORM_B), c1(MSM), ALU.subtract))
            nc.vector.tensor_scalar(shift[:, :], s["ident"][:, :], 0.0, c1(TV), ALU.mult, ALU.add).then_inc(shift_ready, 1)
            dve.wait_ge(row_product, 1)
            nc.vector.tensor_tensor(row[:, :], ps_row[:, :], s["finb"][:, :], ALU.add).then_inc(weights, 1)

            def step(t):
                b = t.back(1)
                if b.within(NB):
                    norm_scale(nc, dve, ln, b.b, b.slot % 2, s["dis"][:, bass.ds(b.b * G, G)])
                if t.within(NB):
                    k = t.slot % 2
                    dve.wait_ge(product, t.b + 1)
                    dve.wait_ge(xc_ready, t.b + 1)
                    if t.past(2):
                        dve.wait_ge(ln.applied, t.b - 1)
                    nc.vector.tensor_tensor(v[:, k], ps_o[k][:, :, :], xc[:, k], ALU.add).then_inc(summed, 1)
                    dve.wait_ge(summed, t.b + 1)
                    norm_stats(nc, dve, ln, t.b, k, v[:, k])
            staggered(dve, NB, 4, 8, 1, step)

        @block.scalar
        def _(act):
            nc.scalar.activation(s["sdeg"][:, :], s["deg"][:, :], ACT.Sqrt).then_inc(roots, 1)
            act.wait_ge(var_ready, 1)
            nc.scalar.activation(c1(SD), c1(V2), ACT.Sqrt, bias=s["eps"][:, 0:1]).then_inc(roots, 1)

            def step(t):
                b = t.back(1)
                if b.within(NB):
                    k = b.slot % 2
                    if b.past(2):
                        act.wait_ge(saved[k], b.q * 32 + (b.slot // 2) * 16)
                    norm_apply(nc, act, ln, b.b, k, o[:, k], v[:, k])
                if t.within(NB):
                    norm_std(nc, act, ln, t.b, t.slot % 2, s["eps"][:, 0:1])
            staggered(act, NB, 4, 8, 1, step)


def edges2(nc, tab, s, EB):
    with ExitStack() as ctx:
        def sb(name, shape, dt=F32):
            return ctx.enter_context(nc.sbuf_tensor(name, shape, dt))

        def ps(name):
            return [ctx.enter_context(nc.psum_tensor(f"{name}{i}", [P, G, P], F32)) for i in range(2)]

        sem = phase_semaphores(nc, ctx, "edges2")

        src_idx, dst_idx = sb("e2_src_idx", [P, 2, G], I32), sb("e2_dst_idx", [P, 2, G], I32)
        rows = sb("e2_rows", [P, 2, G, H])
        run = sb("e2_run", [P, 2, BLK])
        res = sb("e2_res", [P, 2, G, TW])
        ps_x, ps_o = ps("e2_ps_x"), ps("e2_ps_o")
        gathered, scattered = [sem("gathered0"), sem("gathered1")], [sem("scattered0"), sem("scattered1")]
        idx_ready, dst_ready, turned, scanned, product, stored, cleared = (
            sem(n) for n in ("idx_ready", "dst_ready", "turned", "scanned", "product", "stored", "cleared"))
        block = ctx.enter_context(nc.Block())

        @block.gpsimd
        def _(pool):
            wait_values = WaitValues(pool, "edges2", 2)

            def step(t):
                if t.within(EB):
                    ready, freed = wait_values(t.b + 1, t.b - 1)
                    first_wait(pool, idx_ready)
                    pool.wait_ge(idx_ready, ready)
                    if t.past(2):
                        pool.wait_ge(turned, freed)
                    gather(nc, rows[:, t.slot], tab["y2"], src_idx[:, t.slot], gathered[t.slot])
                b = t.back(1)
                if b.within(EB):
                    ready, rows_ready = wait_values(b.b + 1, b.b + 1)
                    first_wait(pool, dst_ready)
                    pool.wait_ge(dst_ready, ready)
                    pool.wait_ge(stored, rows_ready)
                    scatter(nc, tab["narrow"], dst_idx[:, b.slot], res[:, b.slot], scattered[b.slot])
            nc.gpsimd.memset(res[:, :, :, :], 0.0).then_inc(cleared, 1)
            staggered(pool, EB, 2, 4, 1, step)
            for q in range(2):
                pool.wait_ge(scattered[q], 16 * G * EB // 2)

        @block.tensor
        def _(pe):
            def step(t):
                if t.within(EB):
                    pe.wait_ge(gathered[t.slot], t.q * (16 * G) + 16 * G)
                    if t.past(2):
                        pe.wait_ge(scanned, t.b - 1)
                    for j in range(G):
                        i = nc.tensor.transpose(ps_x[t.slot][:, j, :], rows[:, t.slot, j, :], s["ident"][:, :])
                    i.then_inc(turned, 1)
                b = t.back(1)
                if b.within(EB):
                    pe.wait_ge(scanned, b.b + 1)
                    if b.past(2):
                        pe.wait_ge(stored, b.b - 1)
                    for j in range(G):
                        i = nc.tensor.matmul(ps_o[b.slot][:, j, :], run[:, b.slot, tile(j)], s["w2"][:, :],
                                             start=True, stop=True)
                    i.then_inc(product, 1)
            staggered(pe, EB, 2, 4, 1, step)

        @block.vector
        def _(dve):
            def step(t):
                if t.within(EB):
                    if t.past(2):
                        dve.wait_ge(gathered[t.slot], t.q * (16 * G))
                    nc.vector.tensor_copy(src_idx[:, t.slot, :], s["src"][:, bass.ds(t.b * G, G)]).then_inc(idx_ready, 1)
                b = t.back(1)
                if b.within(EB):
                    if b.past(2):
                        dve.wait_ge(scattered[b.slot], b.q * (16 * G))
                        dve.wait_ge(product, b.b - 1)
                    nc.vector.tensor_copy(dst_idx[:, b.slot, :],
                                          s["scat"][:, bass.ds(b.b * G, G)]).then_inc(dst_ready, 1)
                    if b.past(1):
                        dve.wait_ge(scanned, b.b)
                    dve.wait_ge(turned, b.b + 1)
                    nc.vector.tensor_tensor_scan(run[:, b.slot, :], s["mask"][:, bass.ds(b.b * BLK, BLK)],
                                                 ps_x[b.slot][:, :, :].rearrange("p j f -> p (j f)"),
                                                 initial=run[:, 1 - b.slot, BLK - 1:BLK] if b.past(1) else 0.0,
                                                 op0=ALU.mult, op1=ALU.add).then_inc(scanned, 1)
            staggered(dve, EB, 2, 4, 1, step)

        @block.scalar
        def _(act):
            def step(t):
                act.wait_ge(product, t.b + 1)
                if t.past(2):
                    act.wait_ge(scattered[t.slot], t.q * (16 * G))
                nc.scalar.activation(res[:, t.slot, :, 0:H], ps_o[t.slot][:, :, :], ACT.Copy).then_inc(stored, 1)
            act.wait_ge(cleared, 1)
            staggered(act, EB, 2, 4, 0, step)


def nodes2(nc, tab, s, NB):
    with ExitStack() as ctx:
        def sb(name, shape, dt=F32):
            return ctx.enter_context(nc.sbuf_tensor(name, shape, dt))

        def ps(name):
            return [ctx.enter_context(nc.psum_tensor(f"{name}{i}", [P, G, P], F32)) for i in range(2)]

        sem = phase_semaphores(nc, ctx, "nodes2")

        y, w = sb("n2_y", [P, 2, G, H]), sb("n2_w", [P, 4, G, TW])
        yT = sb("n2_yT", [P, 2, BLK])
        x2 = sb("n2_x2", [P, 4, G, H])
        v, o = sb("n2_v", [P, 2, G, H]), sb("n2_o", [P, 2, G, H])
        ps_x, ps_o = ps("n2_ps_x"), ps("n2_ps_o")
        ln = Norm(nc, ctx, sem, "n2_ln")
        y_in, w_in = [sem(f"y_in{i}") for i in range(2)], [sem(f"w_in{i}") for i in range(4)]
        saved = [sem(f"saved{i}") for i in range(2)]
        turned, copied, product, rescaled, biased, summed = (
            sem(n) for n in ("turned", "copied", "product", "rescaled", "biased", "summed"))
        y_v, w_v, o_v = rows_of(tab["y2"]), rows_of(tab["narrow"]), rows_of(tab["x3"])
        block = ctx.enter_context(nc.Block())

        @block.sync
        def _(sp):
            def step(t):
                if t.within(NB):
                    k = t.slot % 2
                    if t.past(2):
                        sp.wait_ge(turned, t.b - 1)
                        sp.wait_ge(rescaled, t.b - 1)
                    sp.dma_start(y[:, k], y_v[t.b]).then_inc(y_in[k], 16)
                    if t.past(4):
                        sp.wait_ge(product, t.b - 3)
                    sp.dma_start(w[:, t.slot], w_v[t.b]).then_inc(w_in[t.slot], 16)
                b = t.back(3)
                if b.within(NB):
                    sp.wait_ge(ln.applied, b.b + 1)
                    sp.dma_start(o_v[b.b], o[:, b.slot % 2]).then_inc(saved[b.slot % 2], 16)
            staggered(sp, NB, 4, 8, 3, step)
            for q in range(2):
                sp.wait_ge(saved[q], 16 * NB // 2)

        @block.gpsimd
        def _(pool):
            def step(t):
                k = t.slot % 2
                pool.wait_ge(y_in[k], t.q * 32 + (t.slot // 2) * 16 + 16)
                if t.past(4):
                    pool.wait_ge(summed, t.b - 3)
                nc.gpsimd.tensor_tensor(x2[:, t.slot], y[:, k], per_node(s["sdeg"][:, bass.ds(t.b * G, G)]),
                                        ALU.mult).then_inc(rescaled, 1)
            staggered(pool, NB, 4, 8, 0, step)

        @block.tensor
        def _(pe):
            def step(t):
                if t.within(NB):
                    k = t.slot % 2
                    pe.wait_ge(y_in[k], t.q * 32 + (t.slot // 2) * 16 + 16)
                    if t.past(2):
                        pe.wait_ge(copied, t.b - 1)
                    for j in range(G):
                        i = nc.tensor.transpose(ps_x[k][:, j, :], y[:, k, j, :], s["ident"][:, :])
                    i.then_inc(turned, 1)
                b = t.back(1)
                if b.within(NB):
                    k = b.slot % 2
                    pe.wait_ge(copied, b.b + 1)
                    pe.wait_ge(w_in[b.slot], b.q * 16 + 16)
                    if b.past(2):
                        pe.wait_ge(biased, b.b - 1)
                    for j in range(G):
                        nc.tensor.matmul(ps_o[k][:, j, :], yT[:, k, tile(j)], s["w2"][:, :], start=True, stop=False)
                        i = nc.tensor.matmul(ps_o[k][:, j, :], s["ident"][:, :], w[:, b.slot, j, 0:H],
                                             start=False, stop=True)
                    i.then_inc(product, 1)
            staggered(pe, NB, 4, 8, 1, step)

        @block.vector
        def _(dve):
            def step(t):
                b = t.back(2)
                if b.within(NB):
                    norm_scale(nc, dve, ln, b.b, b.slot % 2)
                b = t.back(1)
                if b.within(NB):
                    k = b.slot % 2
                    dve.wait_ge(product, b.b + 1)
                    if b.past(2):
                        dve.wait_ge(ln.applied, b.b - 1)
                    for j in range(G):
                        i = nc.vector.scalar_tensor_tensor(v[:, k, j, :], ps_o[k][:, j, :],
                                                           s["dis"][:, bass.ds(b.b * G + j, 1)], s["b2"][:, :],
                                                           ALU.mult, ALU.add)
                    i.then_inc(biased, 1)
                    dve.wait_ge(biased, b.b + 1)
                    dve.wait_ge(rescaled, b.b + 1)
                    nc.vector.scalar_tensor_tensor(v[:, k], v[:, k], 0.0, x2[:, b.slot],
                                                   ALU.max, ALU.add).then_inc(summed, 1)
                    dve.wait_ge(summed, b.b + 1)
                    norm_stats(nc, dve, ln, b.b, k, v[:, k])
            staggered(dve, NB, 4, 8, 2, step)

        @block.scalar
        def _(act):
            def step(t):
                if t.within(NB):
                    k = t.slot % 2
                    act.wait_ge(turned, t.b + 1)
                    if t.past(2):
                        act.wait_ge(product, t.b - 1)
                    nc.scalar.activation(yT[:, k, :], ps_x[k][:, :, :].rearrange("p j f -> p (j f)"),
                                         ACT.Copy).then_inc(copied, 1)
                b = t.back(2)
                if b.within(NB):
                    k = b.slot % 2
                    if b.past(2):
                        act.wait_ge(saved[k], b.q * 32 + (b.slot // 2) * 16)
                    norm_apply(nc, act, ln, b.b, k, o[:, k], v[:, k])
                b = t.back(1)
                if b.within(NB):
                    norm_std(nc, act, ln, b.b, b.slot % 2, s["eps"][:, 0:1])
            staggered(act, NB, 4, 8, 2, step)


def edges3(nc, tab, s, EB):
    with ExitStack() as ctx:
        def sb(name, shape, dt=F32):
            return ctx.enter_context(nc.sbuf_tensor(name, shape, dt))

        def ps(name):
            return [ctx.enter_context(nc.psum_tensor(f"{name}{i}", [P, G, P], F32)) for i in range(2)]

        sem = phase_semaphores(nc, ctx, "edges3")

        src_idx, dst_idx = sb("e3_src_idx", [P, 2, G], I32), sb("e3_dst_idx", [P, 2, G], I32)
        rows, weighted = sb("e3_rows", [P, 2, G, H]), sb("e3_weighted", [P, 2, G, H])
        run = sb("e3_run", [P, 2, BLK])
        v, n = sb("e3_v", [P, 2, G, H]), sb("e3_n", [P, 2, G, H])
        res = sb("e3_res", [P, 2, G, H])
        ps_x, ps_o = ps("e3_ps_x"), ps("e3_ps_o")
        ln = Norm(nc, ctx, sem, "e3_ln")
        gathered, scattered = [sem("gathered0"), sem("gathered1")], [sem("scattered0"), sem("scattered1")]
        idx_ready, dst_ready, scaled, turned, scanned, product, biased, gained, shifted, stored = (
            sem(m) for m in ("idx_ready", "dst_ready", "scaled", "turned", "scanned", "product", "biased", "gained",
                             "shifted", "stored"))
        block = ctx.enter_context(nc.Block())

        @block.gpsimd
        def _(pool):
            wait_values = WaitValues(pool, "edges3", 2)

            def step(t):
                if t.within(EB):
                    ready, freed = wait_values(t.b + 1, t.b - 1)
                    first_wait(pool, idx_ready)
                    pool.wait_ge(idx_ready, ready)
                    if t.past(2):
                        pool.wait_ge(scaled, freed)
                    gather(nc, rows[:, t.slot], tab["x3"], src_idx[:, t.slot], gathered[t.slot])
                b = t.back(3)
                if b.within(EB):
                    ready, rows_ready = wait_values(b.b + 1, b.b + 1)
                    first_wait(pool, dst_ready)
                    pool.wait_ge(dst_ready, ready)
                    pool.wait_ge(stored, rows_ready)
                    scatter(nc, tab["last"], dst_idx[:, b.slot], res[:, b.slot], scattered[b.slot])
            staggered(pool, EB, 2, 6, 3, step)
            for q in range(2):
                pool.wait_ge(scattered[q], 16 * G * EB // 2)

        @block.tensor
        def _(pe):
            def step(t):
                if t.within(EB):
                    pe.wait_ge(scaled, t.b + 1)
                    if t.past(2):
                        pe.wait_ge(scanned, t.b - 1)
                    for j in range(G):
                        i = nc.tensor.transpose(ps_x[t.slot][:, j, :], weighted[:, t.slot, j, :], s["ident"][:, :])
                    i.then_inc(turned, 1)
                b = t.back(1)
                if b.within(EB):
                    pe.wait_ge(scanned, b.b + 1)
                    if b.past(2):
                        pe.wait_ge(biased, b.b - 1)
                    for j in range(G):
                        i = nc.tensor.matmul(ps_o[b.slot][:, j, :], run[:, b.slot, tile(j)], s["w3"][:, :],
                                             start=True, stop=True)
                    i.then_inc(product, 1)
            staggered(pe, EB, 2, 6, 1, step)

        @block.vector
        def _(dve):
            def step(t):
                if t.within(EB):
                    if t.past(2):
                        dve.wait_ge(gathered[t.slot], t.q * (16 * G))
                    nc.vector.tensor_copy(src_idx[:, t.slot, :], s["src"][:, bass.ds(t.b * G, G)]).then_inc(idx_ready, 1)
                b = t.back(3)
                if b.within(EB):
                    k = b.slot
                    dve.wait_ge(ln.applied, b.b + 1)
                    nc.vector.tensor_tensor(n[:, k], n[:, k], to4(s["g3"]), ALU.mult).then_inc(gained, 1)
                    if b.past(2):
                        dve.wait_ge(scattered[k], b.q * (16 * G))
                    nc.vector.tensor_copy(dst_idx[:, k, :], s["scat"][:, bass.ds(b.b * G, G)]).then_inc(dst_ready, 1)
                    dve.wait_ge(gained, b.b + 1)
                    nc.vector.tensor_tensor(n[:, k], n[:, k], to4(s["be3"]), ALU.add).then_inc(shifted, 1)
                b = t.back(2)
                if b.within(EB):
                    k = b.slot
                    dve.wait_ge(product, b.b + 1)
                    if b.past(2):
                        dve.wait_ge(ln.applied, b.b - 1)
                    nc.vector.tensor_tensor(v[:, k], ps_o[k][:, :, :], to4(s["b3"]), ALU.add).then_inc(biased, 1)
                    dve.wait_ge(biased, b.b + 1)
                    norm_stats(nc, dve, ln, b.b, k, v[:, k])
                b = t.back(1)
                if b.within(EB):
                    if b.past(1):
                        dve.wait_ge(scanned, b.b)
                    if b.past(2):
                        dve.wait_ge(product, b.b - 1)
                    dve.wait_ge(turned, b.b + 1)
                    nc.vector.tensor_tensor_scan(run[:, b.slot, :], s["mask"][:, bass.ds(b.b * BLK, BLK)],
                                                 ps_x[b.slot][:, :, :].rearrange("p j f -> p (j f)"),
                                                 initial=run[:, 1 - b.slot, BLK - 1:BLK] if b.past(1) else 0.0,
                                                 op0=ALU.mult, op1=ALU.add).then_inc(scanned, 1)
                b = t.back(2)
                if b.within(EB):
                    norm_scale(nc, dve, ln, b.b, b.slot)
                if t.within(EB):
                    dve.wait_ge(gathered[t.slot], t.q * (16 * G) + 16 * G)
                    if t.past(2):
                        dve.wait_ge(turned, t.b - 1)
                    nc.vector.tensor_tensor(weighted[:, t.slot], rows[:, t.slot],
                                            per_node(s["ew"][:, bass.ds(t.b * G, G)]), ALU.mult).then_inc(scaled, 1)
            staggered(dve, EB, 2, 6, 3, step)

        @block.scalar
        def _(act):
            def step(t):
                b = t.back(3)
                if b.within(EB):
                    k = b.slot
                    act.wait_ge(shifted, b.b + 1)
                    if b.past(2):
                        act.wait_ge(scattered[k], b.q * (16 * G))
                    nc.scalar.activation(res[:, k], n[:, k], ACT.Relu).then_inc(stored, 1)
                b = t.back(2)
                if b.within(EB):
                    k = b.slot
                    norm_std(nc, act, ln, b.b, k, s["eps"][:, 1:2])
                    norm_apply(nc, act, ln, b.b, k, n[:, k], v[:, k])
            staggered(act, EB, 2, 6, 3, step)


def nodes3(nc, tab, s, out, NB, LAST):
    with ExitStack() as ctx:
        def sb(name, shape, dt=F32):
            return ctx.enter_context(nc.sbuf_tensor(name, shape, dt))

        sem = phase_semaphores(nc, ctx, "nodes3")

        x, w = sb("n3_x", [P, 4, G, H]), sb("n3_w", [P, 4, G, H])
        v, o = sb("n3_v", [P, 2, G, H]), sb("n3_o", [P, 2, G, H])
        ln = Norm(nc, ctx, sem, "n3_ln")
        x_in, w_in = ([sem(f"{n}{i}") for i in range(4)] for n in ("x_in", "w_in"))
        saved = [sem(f"saved{i}") for i in range(2)]
        summed = sem("summed")
        x_v, w_v = rows_of(tab["x3"]), rows_of(tab["last"])
        o_v = rows_of(out[0:(NB - 1) * BLK, :])
        o_last = out[(NB - 1) * BLK:(NB - 1) * BLK + LAST, :].rearrange("(p j) f -> p j f", j=G)
        block = ctx.enter_context(nc.Block())

        @block.sync
        def _(sp):
            def step(t):
                if t.within(NB):
                    if t.past(4):
                        sp.wait_ge(summed, t.b - 3)
                    sp.dma_start(x[:, t.slot], x_v[t.b]).then_inc(x_in[t.slot], 16)
                    sp.dma_start(w[:, t.slot], w_v[t.b]).then_inc(w_in[t.slot], 16)
                b = t.back(3)
                if b.within(NB):
                    sp.wait_ge(ln.applied, b.b + 1)
                    if isinstance(b.q, int) and b.b == NB - 1:
                        sp.dma_start(o_last, o[0:LAST // G, b.slot % 2]).then_inc(saved[b.slot % 2], 16)
                    else:
                        sp.dma_start(o_v[b.b], o[:, b.slot % 2]).then_inc(saved[b.slot % 2], 16)
            staggered(sp, NB, 4, 8, 3, step)
            for q in range(2):
                sp.wait_ge(saved[q], 16 * NB // 2)

        @block.vector
        def _(dve):
            def step(t):
                b = t.back(1)
                if b.within(NB):
                    norm_scale(nc, dve, ln, b.b, b.slot % 2)
                if t.within(NB):
                    k = t.slot % 2
                    dve.wait_ge(x_in[t.slot], t.q * 16 + 16)
                    dve.wait_ge(w_in[t.slot], t.q * 16 + 16)
                    if t.past(2):
                        dve.wait_ge(ln.applied, t.b - 1)
                    nc.vector.tensor_tensor(v[:, k], x[:, t.slot], w[:, t.slot], ALU.add).then_inc(summed, 1)
                    dve.wait_ge(summed, t.b + 1)
                    norm_stats(nc, dve, ln, t.b, k, v[:, k])
            staggered(dve, NB, 4, 8, 1, step)

        @block.scalar
        def _(act):
            def step(t):
                b = t.back(1)
                if b.within(NB):
                    k = b.slot % 2
                    if b.past(2):
                        act.wait_ge(saved[k], b.q * 32 + (b.slot // 2) * 16)
                    norm_apply(nc, act, ln, b.b, k, o[:, k], v[:, k])
                if t.within(NB):
                    norm_std(nc, act, ln, t.b, t.slot % 2, s["eps"][:, 0:1])
            staggered(act, NB, 4, 8, 1, step)


def layout(inputs):
    import numpy as np
    n, e = inputs["x"].shape[0], inputs["dst"].shape[0]
    nb = -(-n // (4 * BLK)) * 4
    eb = -(-e // (2 * BLK)) * 2
    pad_e = eb * BLK - e
    arrays = {k: np.ascontiguousarray(v) for k, v in inputs.items()}
    x = np.pad(arrays["x"], ((0, nb * BLK - n), (0, 0)))
    dst = np.concatenate([arrays["dst"], np.full(pad_e, n, arrays["dst"].dtype)])
    src = np.pad(arrays["src"], (0, pad_e))
    edge = np.array([-1], dst.dtype)
    nxt, prev = np.concatenate([dst[1:], edge]), np.concatenate([edge, dst[:-1]])

    def cols(v):
        return np.ascontiguousarray(v.reshape(-1, P).T)
    attr = np.concatenate([arrays["edge_attr_54"].T, arrays["edge_attr_18"].T])
    new = dict(
        x=x, dst_rows=dst, prev_rows=prev, dst_cols=cols(dst), next_cols=cols(nxt), src_cols=cols(src),
        edge_weight_cols=cols(np.pad(arrays["edge_weight"], (0, pad_e))), edge_attr_T=np.pad(attr, ((0, 0), (0, pad_e))),
        lin_T=arrays["L1_gnn_lin_W"].T, lin1_T=arrays["L1_gnn_lin1_W"].T, lin2_T=arrays["L1_gnn_lin2_W"].T,
        f1_W2_T=arrays["L1_gnn_f1_W2"].T, f2_W2_T=arrays["L1_gnn_f2_W2"].T, cat_T=arrays["L1_gnn_cat_W"].T,
        lins_T=arrays["L1_gnn_lins_W"].transpose(0, 2, 1), lins_b_T=arrays["L1_gnn_lins_b"].T,
        final_T=arrays["L1_gnn_final_W"].T)
    for k in AS_THEY_ARE:
        new[k] = arrays[k]
    return {k: np.ascontiguousarray(v) for k, v in new.items()}


AS_THEY_ARE = ["L0_gnn_W", "L0_gnn_b", "L1_gnn_lin_b", "L1_gnn_f1_W1", "L1_gnn_f2_W1", "L1_gnn_conv1_rel_W",
               "L1_gnn_conv1_rel_b", "L1_gnn_conv1_root_W", "L1_gnn_conv2_rel_W", "L1_gnn_conv2_rel_b",
               "L1_gnn_conv2_root_W", "L1_gnn_lin1_b", "L1_gnn_lin2_b", "L1_gnn_cat_b", "L1_gnn_norm_w",
               "L1_gnn_norm_b", "L1_gnn_norm_ms", "L1_gnn_final_b", "L2_gnn_W", "L2_gnn_b", "L3_gnn_W", "L3_gnn_b",
               "L3_gnn_gamma", "L3_gnn_beta"]


def kernel(**inputs):
    import concourse.bacc as bacc
    from concourse.bass_utils import run_bass_kernel_spmd

    arrays = layout(inputs)
    nc = bacc.Bacc("TRN2", target_bir_lowering=False, num_devices=1)
    a = {k: nc.dram_tensor(f"in_{k}", v.shape, mybir.dt.from_np(v.dtype), kind="ExternalInput").ap()
         for k, v in arrays.items()}
    n = inputs["x"].shape[0]
    out = nc.dram_tensor("out", (n, H), F32, kind="ExternalOutput").ap()
    build(nc, a, out, n)
    r = run_bass_kernel_spmd(nc, [{f"in_{k}": v for k, v in arrays.items()}], core_ids=[0])
    return r.results[0]["out"]
```

```python
import concourse.bass as bass
from concourse import mybir
from contextlib import ExitStack


F32 = mybir.dt.float32
BF16 = mybir.dt.bfloat16
I32 = mybir.dt.int32
ALU = mybir.AluOpType
ACT = mybir.ActivationFunctionType

P = 128
H = 128
G = 4
BLK = G * P
F54, F18 = 54, 18
FA = F54 + F18
MID = 64
TW = 132
SKIP = 1 << 17
PENALTY = 3.0e38
LN_EPS = 1e-5
LN3_EPS = 1e-3
GN_EPS = 1e-5


class Turn:

    def __init__(self, q, slot, unroll):
        self.q, self.slot, self.unroll = q, slot, unroll

    @property
    def b(self):
        return self.q * self.unroll + self.slot

    def round(self, ring):
        return self.q * (self.unroll // ring) + self.slot // ring

    def back(self, lag):
        k = self.slot - lag
        return Turn(self.q + k // self.unroll, k % self.unroll, self.unroll)

    def within(self, count):
        return not isinstance(self.q, int) or 0 <= self.b < count

    def past(self, n):
        return not isinstance(self.q, int) or self.b >= n


def staggered(eng, count, unroll, peel, lag, step):
    for t in range(peel):
        step(Turn(t // unroll, t % unroll, unroll))
    with eng.Fori(peel // unroll, count // unroll) as q:
        for u in range(unroll):
            step(Turn(q, u, unroll))
    for t in range(count // unroll * unroll, count + lag):
        step(Turn(t // unroll, t % unroll, unroll))


def phase_semaphores(nc, ctx, phase):
    held = []

    def clear():
        nc.clear_and_free_semaphores(held)
        nc.all_engine_barrier()

    def sem(name):
        held.append(nc.alloc_semaphore(name=f"{phase}_{name}"))
        return held[-1]
    ctx.callback(clear)
    return sem


def first_wait(eng, sem):
    eng.wait_ge(sem, 1)


class WaitValues:

    def __init__(self, eng, phase, count):
        self.eng = eng
        self.regs = [eng.alloc_register(f"{phase}_wait{i}") for i in range(count)]

    def __call__(self, *values):
        if all(isinstance(v, int) for v in values):
            return values
        for reg, v in zip(self.regs, values):
            self.eng.reg_mov(reg, v)
        return self.regs


def build(nc, a, out, n_nodes):
    NB = a["x"].shape[0] // BLK
    EB = a["dst_rows"].shape[0] // BLK
    LAST = n_nodes - (NB - 1) * BLK
    assert NB % 4 == 0 and EB % 2 == 0 and 0 < LAST <= BLK and LAST % G == 0
    assert NB * BLK < SKIP
    NROWS = NB * BLK

    def dram(name, shape, dt=F32):
        return nc.dram_tensor(name, shape, dt, kind="Internal").ap()

    tab = dict(
        narrow=dram("table_narrow", (NROWS, TW)), wide=dram("table_wide", (NROWS, 2 * H)),
        last=dram("table_last", (NROWS, H)), x1=dram("x1_rows", (NROWS, H)), hT=dram("hT", (NB, P, BLK)),
        y2=dram("y2", (NROWS, H)), x3=dram("x3", (NROWS, H)),
        cont=dram("cont_row", (1, EB * BLK), BF16), pen=dram("pen_row", (1, EB * BLK), BF16))

    with ExitStack() as top:
        def sb(name, shape, dt=F32):
            return top.enter_context(nc.sbuf_tensor(name, shape, dt))

        s = dict(
            mask=sb("mask", [P, EB * BLK], BF16),
            src=sb("src_cols", [P, EB * G], I32), scat=sb("scatter_cols", [P, EB * G], I32),
            ew=sb("edge_weight_cols", [P, EB * G]),
            ident=sb("ident", [P, P]), zero=sb("zero", [P, 2048]), eps=sb("eps", [P, 2]), ones=sb("ones", [1, BLK]),
            w0=sb("w0", [P, 2, H]), b0=sb("b0_row", [P, H]),
            lin=sb("lin", [P, H]), A1=sb("A1", [P, H]), R1=sb("R1", [P, H]), A2=sb("A2", [P, H]), R2=sb("R2", [P, H]),
            FW1=sb("FW1", [FA, H]), FW2=sb("FW2", [FA, H]), cat=sb("cat", [P, 2, H]), lins=sb("lins", [P, 3, H]),
            fin=sb("fin", [P, H]), finb=sb("fin_b_row", [P, H]),
            cols=sb("cols", [P, 16]), w2=sb("w2", [P, H]), b2=sb("b2_row", [P, H]), w3=sb("w3", [P, H]),
            b3=sb("b3_row", [P, H]), g3=sb("gamma_row", [P, H]), be3=sb("beta_row", [P, H]),
            default=sb("default_row", [P, G, H]),
            stats=sb("norm_stats", [P, NB, 6]), deg=sb("deg", [P, NB * G]), sdeg=sb("sqrt_deg", [P, NB * G]),
            dis=sb("dis", [P, NB * G]),
        )
        setup(nc, a, tab, s, EB, NB)
        edges0(nc, a, tab, s, EB)
        nodes0(nc, a, tab, s, NB)
        edges1(nc, a, tab, s, EB)
        nodes1(nc, tab, s, NB, LAST)
        norm1(nc, tab, s, NB)
        edges2(nc, tab, s, EB)
        nodes2(nc, tab, s, NB)
        edges3(nc, tab, s, EB)
        nodes3(nc, tab, s, out, NB, LAST)


LIN_B, B1, B2, CAT_B, LS0, LS1, LS2, REL1B, REL2B, L1B, L2B, NORM_W, NORM_B, NORM_MS = range(14)


def setup(nc, a, tab, s, EB, NB):
    with ExitStack() as ctx:
        def sb(name, shape, dt=F32):
            return ctx.enter_context(nc.sbuf_tensor(name, shape, dt))

        sem = phase_semaphores(nc, ctx, "setup")

        dst = sb("dst_cols", [P, EB * G], I32)
        nxt = sb("next_cols", [P, EB * G], I32)
        same = sb("same_as_next", [P, EB * G])
        dst_r = sb("dst_rows", [P, EB * G], I32)
        prv_r = sb("prev_rows", [P, EB * G], I32)
        cont = sb("cont_f32", [P, EB * G])
        cont16 = sb("cont_bf16", [P, EB * G], BF16)
        pen16 = sb("pen_bf16", [P, EB * G], BF16)
        f1w1 = sb("f1w1", [MID, FA])
        f2w1 = sb("f2w1", [MID, FA])
        f1w2, f2w2 = sb("f1w2", [MID, H]), sb("f2w2", [MID, H])
        rel1, root1, rel2, root2 = (sb(n, [P, H]) for n in ("rel1", "root1", "rel2", "root2"))
        lin1, lin2 = sb("lin1", [P, H]), sb("lin2", [P, H])
        d_st, d_mv, d_sd, d_rs = sb("d_st", [P, 6]), sb("d_mv", [P, 2]), sb("d_sd", [P, 1]), sb("d_rs", [P, 1])
        row = sb("row", [P, H])
        ps_w = ctx.enter_context(nc.psum_tensor("ps_w", [P, 4, H], F32))
        ps_f = ctx.enter_context(nc.psum_tensor("ps_f", [FA, 2, H], F32))
        ps_b = ctx.enter_context(nc.psum_tensor("ps_b", [P, 2], F32))

        idx_loaded, mask_loaded, weights_loaded = sem("idx_loaded"), sem("mask_loaded"), sem("weights_loaded")
        pads_cleared, pad_weights = sem("pads_cleared"), sem("pad_weights")
        zeroed, consts, masks, masks_stored, pen_in = (
            sem(n) for n in ("zeroed", "consts", "masks", "masks_stored", "pen_in"))
        table_zeroed, products, chain, std_ready = (
            sem(n) for n in ("table_zeroed", "products", "chain", "std_ready"))

        def col(v):
            return v.rearrange("(p o) -> p o", o=1)

        def row_to_all(v):
            return v.rearrange("(o n) -> o n", o=1).broadcast_to([P, H])

        col_loads = [(LIN_B, "L1_gnn_lin_b"), (CAT_B, "L1_gnn_cat_b"), (REL1B, "L1_gnn_conv1_rel_b"),
                     (REL2B, "L1_gnn_conv2_rel_b"), (L1B, "L1_gnn_lin1_b"), (L2B, "L1_gnn_lin2_b"),
                     (NORM_W, "L1_gnn_norm_w"), (NORM_B, "L1_gnn_norm_b"), (NORM_MS, "L1_gnn_norm_ms")]
        loads = [(s["w0"][:, :, :], a["L0_gnn_W"].rearrange("(s k) o -> k s o", s=2)),
                 (s["lin"][:, :], a["lin_T"]), (s["cat"][:, :, :], a["cat_T"].rearrange("(s k) o -> k s o", s=2)),
                 (s["fin"][:, :], a["final_T"]), (s["w2"][:, :], a["L2_gnn_W"]), (s["w3"][:, :], a["L3_gnn_W"]),
                 (rel1[:, :], a["L1_gnn_conv1_rel_W"]), (root1[:, :], a["L1_gnn_conv1_root_W"]),
                 (rel2[:, :], a["L1_gnn_conv2_rel_W"]), (root2[:, :], a["L1_gnn_conv2_root_W"]),
                 (lin1[:, :], a["lin1_T"]), (lin2[:, :], a["lin2_T"]),
                 (f1w2[:, :], a["f1_W2_T"]), (f2w2[:, :], a["f2_W2_T"]),
                 (s["lins"][:, :, :], a["lins_T"].rearrange("l k m -> k l m")),
                 (s["cols"][:, LS0:LS2 + 1], a["lins_b_T"]),
                 (s["b0"][:, :], row_to_all(a["L0_gnn_b"])), (s["finb"][:, :], row_to_all(a["L1_gnn_final_b"])),
                 (s["b2"][:, :], row_to_all(a["L2_gnn_b"])), (s["b3"][:, :], row_to_all(a["L3_gnn_b"])),
                 (s["g3"][:, :], row_to_all(a["L3_gnn_gamma"])), (s["be3"][:, :], row_to_all(a["L3_gnn_beta"]))]
        loads += [(s["cols"][:, c:c + 1], col(a[n])) for c, n in col_loads]

        block = ctx.enter_context(nc.Block())

        @block.sync
        def _(sp):
            for dst_ap, v in ((dst_r, "dst_rows"), (prv_r, "prev_rows")):
                sp.dma_start(dst_ap[:, :], a[v].rearrange("(p t) -> p t", p=P)).then_inc(mask_loaded, 16)
            sp.wait_ge(zeroed, 1)
            flat = tab["narrow"].rearrange("(p r) c -> p (r c)", p=P)
            width = flat.shape[1]
            step = 1980
            for c in range(0, width, step):
                w = min(step, width - c)
                sp.dma_start(flat[:, c:c + w], s["zero"][:, 0:w]).then_inc(table_zeroed, 16)
            n = -(-width // step)
            sp.wait_ge(table_zeroed, 16 * n)

        @block.scalar
        def _(act):
            for dst_ap, v in ((dst, "dst_cols"), (nxt, "next_cols"), (s["src"], "src_cols")):
                act.dma_start(dst_ap[:, :], a[v]).then_inc(idx_loaded, 16)
            act.dma_start(s["ew"][:, :], a["edge_weight_cols"]).then_inc(idx_loaded, 16)
            for d, v in loads:
                act.dma_start(d, v).then_inc(weights_loaded, 16)
            act.wait_ge(pads_cleared, 2)
            act.dma_start(f1w1[:, 0:F54], a["L1_gnn_f1_W1"]).then_inc(pad_weights, 16)
            act.dma_start(f2w1[:, F54:FA], a["L1_gnn_f2_W1"]).then_inc(pad_weights, 16)
            act.wait_ge(masks, 3)
            act.dma_start(tab["cont"].rearrange("o (p t) -> (o p) t", p=P), cont16[:, :]).then_inc(masks_stored, 16)
            act.dma_start(tab["pen"].rearrange("o (p t) -> (o p) t", p=P), pen16[:, :]).then_inc(masks_stored, 16)
            act.wait_ge(masks_stored, 32)
            act.dma_start(s["mask"][:, :], tab["pen"].broadcast_to([P, EB * BLK]),
                          max_dma_last_dim=16384).then_inc(pen_in, 16)
            act.wait_ge(chain, 2)
            act.wait_ge(consts, 6)
            nc.scalar.activation(d_sd[:, :], d_mv[:, 1:2], ACT.Sqrt, bias=s["eps"][:, 1:2]).then_inc(std_ready, 1)
            act.wait_ge(idx_loaded, 64)
            act.wait_ge(pen_in, 16)

        @block.gpsimd
        def _(pool):
            nc.gpsimd.memset(s["zero"][:, :], 0.0).then_inc(zeroed, 1)
            nc.gpsimd.memset(f1w1[:, :], 0.0).then_inc(pads_cleared, 1)
            nc.gpsimd.memset(f2w1[:, :], 0.0).then_inc(pads_cleared, 1)
            nc.gpsimd.memset(s["ident"][:, :], 0.0).then_inc(consts, 1)
            nc.gpsimd.memset(s["eps"][:, 0:1], LN_EPS).then_inc(consts, 1)
            nc.gpsimd.memset(s["eps"][:, 1:2], LN3_EPS).then_inc(consts, 1)
            nc.gpsimd.memset(s["ones"][:, :], 1.0).then_inc(consts, 1)
            nc.gpsimd.memset(s["cols"][:, 14:16], 0.0).then_inc(consts, 1)
            pool.wait_ge(consts, 5)
            nc.gpsimd.affine_select(out=s["ident"][:, :], in_=s["ident"][:, :], compare_op=ALU.not_equal, fill=1.0,
                                    base=0, pattern=[[-1, P]], channel_multiplier=1).then_inc(consts, 1)

        @block.tensor
        def _(pe):
            pe.wait_ge(weights_loaded, 16 * len(loads))
            pe.wait_ge(pad_weights, 32)
            nc.tensor.matmul(ps_w[:, 0, :], rel1[:, :], lin1[:, :], start=True, stop=True)
            nc.tensor.matmul(ps_w[:, 1, :], root1[:, :], lin1[:, :], start=True, stop=True)
            nc.tensor.matmul(ps_w[:, 2, :], rel2[:, :], lin2[:, :], start=True, stop=True)
            nc.tensor.matmul(ps_w[:, 3, :], root2[:, :], lin2[:, :], start=True, stop=True)
            nc.tensor.matmul(ps_f[:, 0, :], f1w1[:, :], f1w2[:, :], start=True, stop=True)
            nc.tensor.matmul(ps_f[:, 1, :], f2w1[:, :], f2w2[:, :], start=True, stop=True)
            nc.tensor.matmul(ps_b[:, 0:1], lin1[:, :], s["cols"][:, REL1B:REL1B + 1], start=True, stop=True)
            nc.tensor.matmul(ps_b[:, 1:2], lin2[:, :], s["cols"][:, REL2B:REL2B + 1],
                             start=True, stop=True).then_inc(products, 1)

        @block.vector
        def _(dve):
            dve.wait_ge(mask_loaded, 32)
            nc.vector.tensor_tensor(cont[:, :], dst_r[:, :], prv_r[:, :], ALU.is_equal).then_inc(masks, 1)
            dve.wait_ge(masks, 1)
            nc.vector.tensor_copy(cont16[:, :], cont[:, :]).then_inc(masks, 1)
            nc.vector.tensor_scalar(pen16[:, :], cont[:, :], -PENALTY, PENALTY, ALU.mult, ALU.add).then_inc(masks, 1)
            dve.wait_ge(idx_loaded, 64)
            nc.vector.tensor_tensor(same[:, :], dst[:, :], nxt[:, :], ALU.is_equal).then_inc(masks, 1)
            dve.wait_ge(masks, 4)
            nc.vector.scalar_tensor_tensor(s["scat"][:, :], same[:, :], float(SKIP), dst[:, :],
                                           ALU.mult, ALU.add).then_inc(masks, 1)
            dve.wait_ge(weights_loaded, 16 * len(loads))
            nc.vector.bn_stats(d_st[:, :], s["b3"][:, :]).then_inc(chain, 1)
            dve.wait_ge(chain, 1)
            nc.vector.bn_aggr(d_mv[:, :], d_st[:, :]).then_inc(chain, 1)
            dve.wait_ge(std_ready, 1)
            nc.vector.reciprocal(d_rs[:, :], d_sd[:, :]).then_inc(chain, 1)
            dve.wait_ge(chain, 3)
            nc.vector.tensor_scalar(row[:, :], s["b3"][:, :], d_mv[:, 0:1], d_rs[:, :],
                                    ALU.subtract, ALU.mult).then_inc(chain, 1)
            dve.wait_ge(chain, 4)
            nc.vector.tensor_tensor(row[:, :], row[:, :], s["g3"][:, :], ALU.mult).then_inc(chain, 1)
            dve.wait_ge(chain, 5)
            nc.vector.tensor_tensor(row[:, :], row[:, :], s["be3"][:, :], ALU.add).then_inc(chain, 1)
            dve.wait_ge(chain, 6)
            for j in range(G):
                nc.vector.tensor_scalar_max(s["default"][:, j, :], row[:, :], 0.0)
            dve.wait_ge(products, 1)
            for i, n in enumerate(("A1", "R1", "A2", "R2")):
                nc.vector.tensor_copy(s[n][:, :], ps_w[:, i, :])
            nc.vector.tensor_copy(s["FW1"][:, :], ps_f[:, 0, :])
            nc.vector.tensor_copy(s["FW2"][:, :], ps_f[:, 1, :])
            nc.vector.tensor_tensor(s["cols"][:, B1:B1 + 1], ps_b[:, 0:1], s["cols"][:, L1B:L1B + 1], ALU.add)
            nc.vector.tensor_tensor(s["cols"][:, B2:B2 + 1], ps_b[:, 1:2], s["cols"][:, L2B:L2B + 1], ALU.add)


def rows_of(table):
    return table.rearrange("(b p j) f -> b p (j f)", p=P, j=G)


def gather(nc, rows, table, idx, sem):
    for j in range(G):
        nc.gpsimd.indirect_dma_start(out=rows[:, j, :], out_offset=None, in_=table,
                                     in_offset=bass.IndirectOffsetOnAxis(ap=idx[:, j:j + 1], axis=0)).then_inc(sem, 16)


def scatter(nc, table, idx, rows, sem):
    for j in range(G):
        nc.gpsimd.indirect_dma_start(out=table, out_offset=bass.IndirectOffsetOnAxis(ap=idx[:, j:j + 1], axis=0),
                                     in_=rows[:, j, :], in_offset=None, bounds_check=table.shape[0] - 1,
                                     oob_is_err=False).then_inc(sem, 16)


def tile(j):
    return slice(j * P, (j + 1) * P)


def edges0(nc, a, tab, s, EB):
    with ExitStack() as ctx:
        def sb(name, shape, dt=F32):
            return ctx.enter_context(nc.sbuf_tensor(name, shape, dt))

        def ps(name):
            return [ctx.enter_context(nc.psum_tensor(f"{name}{i}", [P, G, P], F32)) for i in range(2)]

        sem = phase_semaphores(nc, ctx, "edges0")

        src_idx, dst_idx = sb("e0_src_idx", [P, 2, G], I32), sb("e0_dst_idx", [P, 2, G], I32)
        rows = sb("e0_rows", [P, 2, G, H])
        run = sb("e0_run", [P, 2, BLK])
        cont = sb("e0_cont", [1, 2, BLK], BF16)
        cnt = sb("e0_cnt", [1, 2, BLK])
        res = sb("e0_res", [P, 2, G, TW])
        ps_x, ps_r, ps_c = ps("e0_ps_x"), ps("e0_ps_r"), ps("e0_ps_c")
        gathered, scattered = [sem("gathered0"), sem("gathered1")], [sem("scattered0"), sem("scattered1")]
        cont_in = [sem("cont_in0"), sem("cont_in1")]
        idx_ready, dst_ready, turned, scanned, counted, back, stored, cleared, wide_zeroed = (
            sem(n) for n in ("idx_ready", "dst_ready", "turned", "scanned", "counted", "back", "stored", "cleared",
                             "wide_zeroed"))
        wide_flat = tab["wide"].rearrange("(c p r) f -> c p (r f)", c=EB, p=P)
        assert wide_flat.shape[2] <= 4096
        block = ctx.enter_context(nc.Block())

        @block.sync
        def _(sp):
            def step(t):
                if t.past(2):
                    sp.wait_ge(counted, t.b - 1)
                sp.dma_start(cont[:, t.slot, :], tab["cont"][:, bass.ds(t.b * BLK, BLK)]).then_inc(cont_in[t.slot], 16)
                half = wide_flat.shape[2]
                for c in range(0, half, 2048):
                    w = min(2048, half - c)
                    sp.dma_start(wide_flat[t.b][:, c:c + w], s["zero"][:, 0:w]).then_inc(wide_zeroed, 16)
            staggered(sp, EB, 2, 4, 0, step)
            sp.wait_ge(wide_zeroed, 16 * EB * -(-wide_flat.shape[2] // 2048))

        @block.gpsimd
        def _(pool):
            wait_values = WaitValues(pool, "edges0", 2)

            def step(t):
                if t.within(EB):
                    ready, freed = wait_values(t.b + 1, t.b - 1)
                    first_wait(pool, idx_ready)
                    pool.wait_ge(idx_ready, ready)
                    if t.past(2):
                        pool.wait_ge(turned, freed)
                    gather(nc, rows[:, t.slot], a["x"], src_idx[:, t.slot], gathered[t.slot])
                b = t.back(2)
                if b.within(EB):
                    ready, rows_ready = wait_values(b.b + 1, b.b + 1)
                    first_wait(pool, dst_ready)
                    pool.wait_ge(dst_ready, ready)
                    pool.wait_ge(stored, rows_ready)
                    scatter(nc, tab["narrow"], dst_idx[:, b.slot], res[:, b.slot], scattered[b.slot])
            nc.gpsimd.memset(res[:, :, :, :], 0.0).then_inc(cleared, 1)
            staggered(pool, EB, 2, 4, 2, step)
            for q in range(2):
                pool.wait_ge(scattered[q], 16 * G * EB // 2)

        @block.tensor
        def _(pe):
            def step(t):
                if t.within(EB):
                    pe.wait_ge(gathered[t.slot], t.q * (16 * G) + 16 * G)
                    if t.past(2):
                        pe.wait_ge(scanned, t.b - 1)
                    for j in range(G):
                        i = nc.tensor.transpose(ps_x[t.slot][:, j, :], rows[:, t.slot, j, :], s["ident"][:, :])
                    i.then_inc(turned, 1)
                b = t.back(1)
                if b.within(EB):
                    pe.wait_ge(scanned, b.b + 1)
                    pe.wait_ge(counted, b.b + 1)
                    if b.past(2):
                        pe.wait_ge(stored, b.b - 1)
                    for j in range(G):
                        nc.tensor.transpose(ps_r[b.slot][:, j, :], run[:, b.slot, tile(j)], s["ident"][:, :])
                    for j in range(G):
                        i = nc.tensor.matmul(ps_c[b.slot][:, 0, j:j + 1], cnt[:, b.slot, tile(j)], s["ones"][:, 0:1],
                                             start=True, stop=True)
                    i.then_inc(back, 1)
            staggered(pe, EB, 2, 4, 1, step)

        @block.vector
        def _(dve):
            def copy_idx(t):
                if t.past(2):
                    dve.wait_ge(gathered[t.slot], t.q * (16 * G))
                nc.vector.tensor_copy(src_idx[:, t.slot, :], s["src"][:, bass.ds(t.b * G, G)]).then_inc(idx_ready, 1)

            def step(t):
                if t.within(EB):
                    copy_idx(t)
                b = t.back(1)
                if b.within(EB):
                    if b.past(2):
                        dve.wait_ge(scattered[b.slot], b.q * (16 * G))
                    nc.vector.tensor_copy(dst_idx[:, b.slot, :],
                                          s["scat"][:, bass.ds(b.b * G, G)]).then_inc(dst_ready, 1)
                    if b.past(2):
                        dve.wait_ge(back, b.b - 1)
                    if b.past(1):
                        dve.wait_ge(counted, b.b)
                        dve.wait_ge(scanned, b.b)
                    dve.wait_ge(cont_in[b.slot], b.q * 16 + 16)
                    prev = 1 - b.slot
                    nc.vector.tensor_tensor_scan(cnt[:, b.slot, :], cont[:, b.slot, :], s["ones"][:, :],
                                                 initial=cnt[:, prev, BLK - 1:BLK] if b.past(1) else 0.0,
                                                 op0=ALU.mult, op1=ALU.add).then_inc(counted, 1)
                    dve.wait_ge(turned, b.b + 1)
                    nc.vector.tensor_tensor_scan(run[:, b.slot, :], s["mask"][:, bass.ds(b.b * BLK, BLK)],
                                                 ps_x[b.slot][:, :, :].rearrange("p j f -> p (j f)"),
                                                 initial=run[:, prev, BLK - 1:BLK] if b.past(1) else 0.0,
                                                 op0=ALU.add, op1=ALU.min).then_inc(scanned, 1)
            staggered(dve, EB, 2, 4, 1, step)

        @block.scalar
        def _(act):
            def step(t):
                act.wait_ge(back, t.b + 1)
                if t.past(2):
                    act.wait_ge(scattered[t.slot], t.q * (16 * G))
                nc.scalar.activation(res[:, t.slot, :, 0:H], ps_r[t.slot][:, :, :], ACT.Copy)
                nc.scalar.activation(res[:, t.slot, :, H], ps_c[t.slot][:, 0, 0:G], ACT.Copy).then_inc(stored, 1)
            act.wait_ge(cleared, 1)
            staggered(act, EB, 2, 4, 0, step)


def to4(row):
    return row[:, :].unsqueeze(1).broadcast_to([P, G, H])


def per_node(v):
    return v.unsqueeze(2).broadcast_to([P, G, H])


class Norm:

    def __init__(self, nc, ctx, sem, name="ln"):
        def sb(n, shape):
            return ctx.enter_context(nc.sbuf_tensor(f"{name}_{n}", shape, F32))

        self.st, self.mv = sb("st", [P, 8, G, 6]), sb("mv", [P, 8, G, 2])
        self.sd, self.rs, self.nm = sb("sd", [P, 8, G]), sb("rs", [P, 8, G]), sb("nm", [P, 8, G])
        self.stats_done, self.moments, self.std, self.inv, self.scale_ready, self.applied = (
            sem(f"{name}_{n}") for n in ("stats", "moments", "std", "inv", "scale", "applied"))


def norm_stats(nc, ln, k, v):
    for j in range(G):
        i = nc.vector.bn_stats(ln.st[:, k, j, :], v[:, j, :])
    i.then_inc(ln.stats_done, 1)


def norm_moments(nc, dve, ln, wait_values, b, k):
    done, = wait_values(b + 1)
    first_wait(dve, ln.stats_done)
    dve.wait_ge(ln.stats_done, done)
    for j in range(G):
        i = nc.vector.bn_aggr(ln.mv[:, k, j, :], ln.st[:, k, j, :])
    i.then_inc(ln.moments, 1)


def norm_std(nc, act, ln, b, k, eps):
    act.wait_ge(ln.moments, b + 1)
    nc.scalar.activation(ln.sd[:, k, :], ln.mv[:, k, :, 1], ACT.Sqrt, bias=eps).then_inc(ln.std, 1)


def norm_inverse(nc, dve, ln, b, k):
    dve.wait_ge(ln.std, b + 1)
    nc.vector.reciprocal(ln.rs[:, k, :], ln.sd[:, k, :]).then_inc(ln.inv, 1)


def norm_times(nc, dve, ln, b, k, factor):
    dve.wait_ge(ln.inv, b * 2 + 1)
    nc.vector.tensor_tensor(ln.rs[:, k, :], ln.rs[:, k, :], factor, ALU.mult).then_inc(ln.inv, 1)


def norm_shift(nc, dve, ln, b, k, steps=1):
    dve.wait_ge(ln.inv, b * steps + steps)
    nc.vector.scalar_tensor_tensor(ln.nm[:, k, :], ln.mv[:, k, :, 0], -1.0, ln.rs[:, k, :],
                                   ALU.mult, ALU.mult).then_inc(ln.scale_ready, 1)


def norm_apply(nc, act, ln, b, k, dst, v):
    act.wait_ge(ln.scale_ready, b + 1)
    for j in range(G):
        i = nc.scalar.activation(dst[:, j, :], v[:, j, :], ACT.Identity, bias=ln.nm[:, k, j:j + 1],
                                 scale=ln.rs[:, k, j:j + 1])
    i.then_inc(ln.applied, 1)


def nodes0(nc, a, tab, s, NB):
    with ExitStack() as ctx:
        def sb(name, shape, dt=F32):
            return ctx.enter_context(nc.sbuf_tensor(name, shape, dt))

        def ps(name):
            return [ctx.enter_context(nc.psum_tensor(f"{name}{i}", [P, G, P], F32)) for i in range(2)]

        sem = phase_semaphores(nc, ctx, "nodes0")

        x = sb("n0_x", [P, 8, G, H])
        t0 = sb("n0_t", [P, 4, G, TW])
        has = sb("n0_has", [P, 2, G])
        md = sb("n0_md", [P, 2, G, H])
        xT, mdT = sb("n0_xT", [P, 2, BLK]), sb("n0_mdT", [P, 2, BLK])
        v = sb("n0_v", [P, 8, G, H])
        o = sb("n0_o", [P, 4, G, H])
        ps_x, ps_m, ps_o = ps("n0_ps_x"), ps("n0_ps_m"), ps("n0_ps_o")
        ln = Norm(nc, ctx, sem)
        x_in, t_in = [sem(f"x_in{i}") for i in range(8)], [sem(f"t_in{i}") for i in range(4)]
        saved = [sem(f"saved{i}") for i in range(4)]
        mask_in, has_ready, masked, md_ready, x_turned, md_turned, x_copied, md_copied, product, biased, summed = (
            sem(n) for n in ("mask_in", "has_ready", "masked", "md_ready", "x_turned", "md_turned", "x_copied",
                             "md_copied", "product", "biased", "summed"))
        x_v, t_v, o_v = rows_of(a["x"]), rows_of(tab["narrow"]), rows_of(tab["x1"])
        block = ctx.enter_context(nc.Block())

        @block.sync
        def _(sp):
            def step(t):
                if t.within(NB):
                    if t.past(8):
                        sp.wait_ge(summed, t.b - 7)
                    sp.dma_start(x[:, t.slot], x_v[t.b]).then_inc(x_in[t.slot], 16)
                    if t.past(4):
                        sp.wait_ge(md_ready, t.b - 3)
                    sp.dma_start(t0[:, t.slot % 4], t_v[t.b]).then_inc(t_in[t.slot % 4], 16)
            sp.dma_start(s["mask"][:, :], tab["cont"].broadcast_to([P, s["mask"].shape[1]]),
                         max_dma_last_dim=16384).then_inc(mask_in, 16)
            staggered(sp, NB, 8, 16, 0, step)
            sp.wait_ge(mask_in, 16)

        @block.vector
        def _(dve):
            wait_values = WaitValues(dve, "nodes0_dve", 1)
            def step(t):
                if t.within(NB):
                    k = t.slot % 2
                    dve.wait_ge(t_in[t.slot % 4], t.round(4) * 16 + 16)
                    if t.past(2):
                        dve.wait_ge(masked, t.b - 1)
                    nc.vector.tensor_scalar_min(has[:, k, :], t0[:, t.slot % 4, :, H], 1.0).then_inc(has_ready, 1)
                    nc.vector.tensor_scalar_add(s["deg"][:, bass.ds(t.b * G, G)], t0[:, t.slot % 4, :, H],
                                                1.0).then_inc(has_ready, 1)
                b = t.back(8)
                if b.within(NB):
                    norm_inverse(nc, dve, ln, b.b, b.slot)
                b = t.back(3)
                if b.within(NB):
                    k, n = b.slot % 2, b.slot
                    dve.wait_ge(product, b.b + 1)
                    if b.past(8):
                        dve.wait_ge(ln.applied, b.b - 7)
                    nc.vector.tensor_tensor(v[:, n], ps_o[k][:, :, :], to4(s["b0"]), ALU.add).then_inc(biased, 1)
                b = t.back(6)
                if b.within(NB):
                    norm_moments(nc, dve, ln, wait_values, b.b, b.slot)
                b = t.back(4)
                if b.within(NB):
                    n = b.slot
                    dve.wait_ge(biased, b.b + 1)
                    nc.vector.scalar_tensor_tensor(v[:, n], v[:, n], 0.0, x[:, n], ALU.max, ALU.add).then_inc(summed, 1)
                b = t.back(5)
                if b.within(NB):
                    n = b.slot
                    dve.wait_ge(summed, b.b + 1)
                    norm_stats(nc, ln, n, v[:, n])
                b = t.back(8)
                if b.within(NB):
                    norm_shift(nc, dve, ln, b.b, b.slot)
            staggered(dve, NB, 8, 16, 8, step)

        @block.gpsimd
        def _(pool):
            def step(t):
                k = t.slot % 2
                pool.wait_ge(x_in[t.slot], t.q * 16 + 16)
                pool.wait_ge(has_ready, t.b * 2 + 2)
                if t.past(2):
                    pool.wait_ge(md_turned, t.b - 1)
                nc.gpsimd.tensor_tensor(md[:, k], x[:, t.slot], per_node(has[:, k, :]), ALU.mult).then_inc(masked, 1)
                pool.wait_ge(masked, t.b + 1)
                nc.gpsimd.tensor_tensor(md[:, k], md[:, k], t0[:, t.slot % 4, :, 0:H], ALU.subtract).then_inc(md_ready, 1)
            staggered(pool, NB, 8, 16, 0, step)

        @block.tensor
        def _(pe):
            def step(t):
                if t.within(NB):
                    k = t.slot % 2
                    pe.wait_ge(x_in[t.slot], t.q * 16 + 16)
                    if t.past(2):
                        pe.wait_ge(x_copied, t.b - 1)
                    for j in range(G):
                        i = nc.tensor.transpose(ps_x[k][:, j, :], x[:, t.slot, j, :], s["ident"][:, :])
                    i.then_inc(x_turned, 1)
                b = t.back(1)
                if b.within(NB):
                    k = b.slot % 2
                    pe.wait_ge(md_ready, b.b + 1)
                    if b.past(2):
                        pe.wait_ge(md_copied, b.b - 1)
                    for j in range(G):
                        i = nc.tensor.transpose(ps_m[k][:, j, :], md[:, k, j, :], s["ident"][:, :])
                    i.then_inc(md_turned, 1)
                b = t.back(2)
                if b.within(NB):
                    k = b.slot % 2
                    pe.wait_ge(x_copied, b.b + 1)
                    pe.wait_ge(md_copied, b.b + 1)
                    if b.past(2):
                        pe.wait_ge(biased, b.b - 1)
                    for j in range(G):
                        nc.tensor.matmul(ps_o[k][:, j, :], xT[:, k, tile(j)], s["w0"][:, 0, :], start=True, stop=False)
                        i = nc.tensor.matmul(ps_o[k][:, j, :], mdT[:, k, tile(j)], s["w0"][:, 1, :],
                                             start=False, stop=True)
                    i.then_inc(product, 1)
            staggered(pe, NB, 8, 16, 2, step)

        @block.scalar
        def _(act):
            def step(t):
                b = t.back(9)
                if b.within(NB):
                    act.wait_ge(ln.applied, b.b + 1)
                    act.dma_start(o_v[b.b], o[:, b.slot % 4]).then_inc(saved[b.slot % 4], 16)
                if t.within(NB):
                    k = t.slot % 2
                    act.wait_ge(x_turned, t.b + 1)
                    if t.past(2):
                        act.wait_ge(product, t.b - 1)
                    nc.scalar.activation(xT[:, k, :], ps_x[k][:, :, :].rearrange("p j f -> p (j f)"),
                                         ACT.Copy).then_inc(x_copied, 1)
                b = t.back(1)
                if b.within(NB):
                    k = b.slot % 2
                    act.wait_ge(md_turned, b.b + 1)
                    if b.past(2):
                        act.wait_ge(product, b.b - 1)
                    nc.scalar.activation(mdT[:, k, :], ps_m[k][:, :, :].rearrange("p j f -> p (j f)"),
                                         ACT.Copy).then_inc(md_copied, 1)
                b = t.back(6)
                if b.within(NB):
                    norm_std(nc, act, ln, b.b, b.slot, s["eps"][:, 0:1])
                b = t.back(8)
                if b.within(NB):
                    k = b.slot % 4
                    if b.past(4):
                        act.wait_ge(saved[k], b.round(4) * 16)
                    norm_apply(nc, act, ln, b.b, b.slot, o[:, k], v[:, b.slot])
            staggered(act, NB, 8, 16, 9, step)
            for q in range(4):
                act.wait_ge(saved[q], 16 * NB // 4)


def edges1(nc, a, tab, s, EB):
    with ExitStack() as ctx:
        def sb(name, shape, dt=F32):
            return ctx.enter_context(nc.sbuf_tensor(name, shape, dt))

        def ps(name):
            return ctx.enter_context(nc.psum_tensor(name, [P, G, P], F32))

        sem = phase_semaphores(nc, ctx, "edges1")

        src_idx, dst_idx = sb("e1_src_idx", [P, 2, G], I32), sb("e1_dst_idx", [P, 2, G], I32)
        rows = sb("e1_rows", [P, 2, G, H])
        ea = sb("e1_ea", [FA, 2, BLK])
        xT, xs = sb("e1_xT", [P, 2, BLK]), sb("e1_xs", [P, 2, BLK])
        m1, m2 = sb("e1_m1", [P, BLK]), sb("e1_m2", [P, BLK])
        run1, run2 = sb("e1_run1", [P, 2, BLK]), sb("e1_run2", [P, 2, BLK])
        res = sb("e1_res", [P, 2, G, 2 * H])
        ps_x, ps_l, ps_f1, ps_f2, ps_o1, ps_o2 = (ps(f"e1_ps{i}") for i in range(6))
        gathered, scattered = [sem("gathered0"), sem("gathered1")], [sem("scattered0"), sem("scattered1")]
        ea_in = [sem("ea_in0"), sem("ea_in1")]
        idx_ready, dst_ready, turned, copied, lined, active, f_ready, mul1, mul2, scanned1, scanned2, product, stored = (
            sem(n) for n in ("idx_ready", "dst_ready", "turned", "copied", "lined", "active", "f_ready", "mul1", "mul2",
                             "scanned1", "scanned2", "product", "stored"))

        def flat(bank):
            return bank[:, :, :].rearrange("p j f -> p (j f)")
        block = ctx.enter_context(nc.Block())

        @block.sync
        def _(sp):
            def step(t):
                if t.past(2):
                    sp.wait_ge(f_ready, t.b - 1)
                sp.dma_start(ea[:, t.slot, :], a["edge_attr_T"][:, bass.ds(t.b * BLK, BLK)]).then_inc(ea_in[t.slot], 16)
            staggered(sp, EB, 2, 4, 0, step)

        @block.gpsimd
        def _(pool):
            wait_values = WaitValues(pool, "edges1", 2)

            def step(t):
                if t.within(EB):
                    ready, freed = wait_values(t.b + 1, t.b - 1)
                    first_wait(pool, idx_ready)
                    pool.wait_ge(idx_ready, ready)
                    if t.past(2):
                        pool.wait_ge(turned, freed)
                    gather(nc, rows[:, t.slot], tab["x1"], src_idx[:, t.slot], gathered[t.slot])
                b = t.back(3)
                if b.within(EB):
                    ready, rows_ready = wait_values(b.b + 1, b.b * 2 + 2)
                    first_wait(pool, dst_ready)
                    pool.wait_ge(dst_ready, ready)
                    pool.wait_ge(stored, rows_ready)
                    scatter(nc, tab["wide"], dst_idx[:, b.slot], res[:, b.slot], scattered[b.slot])
            staggered(pool, EB, 2, 6, 3, step)
            for q in range(2):
                pool.wait_ge(scattered[q], 16 * G * EB // 2)

        @block.tensor
        def _(pe):
            def step(t):
                if t.within(EB):
                    pe.wait_ge(gathered[t.slot], t.q * (16 * G) + 16 * G)
                    if t.past(1):
                        pe.wait_ge(copied, t.b)
                    for j in range(G):
                        i = nc.tensor.transpose(ps_x[:, j, :], rows[:, t.slot, j, :], s["ident"][:, :])
                    i.then_inc(turned, 1)
                    pe.wait_ge(ea_in[t.slot], t.q * 16 + 16)
                    if t.past(1):
                        pe.wait_ge(mul2, t.b)
                    nc.tensor.matmul(flat(ps_f1), s["FW1"][:, :], ea[:, t.slot, :], start=True, stop=True)
                    nc.tensor.matmul(flat(ps_f2), s["FW2"][:, :], ea[:, t.slot, :],
                                     start=True, stop=True).then_inc(f_ready, 1)
                    pe.wait_ge(copied, t.b + 1)
                    if t.past(1):
                        pe.wait_ge(active, t.b)
                    nc.tensor.matmul(flat(ps_l), s["lin"][:, :], xT[:, t.slot, :], start=True, stop=True).then_inc(lined, 1)
                b = t.back(1)
                if b.within(EB):
                    pe.wait_ge(scanned1, b.b + 1)
                    pe.wait_ge(scanned2, b.b + 1)
                    if b.past(1):
                        pe.wait_ge(stored, b.b * 2)
                    for j in range(G):
                        nc.tensor.matmul(ps_o1[:, j, :], run1[:, b.slot, tile(j)], s["A1"][:, :], start=True, stop=True)
                    for j in range(G):
                        i = nc.tensor.matmul(ps_o2[:, j, :], run2[:, b.slot, tile(j)], s["A2"][:, :],
                                             start=True, stop=True)
                    i.then_inc(product, 1)
            staggered(pe, EB, 2, 4, 1, step)

        @block.scalar
        def _(act):
            def step(t):
                if t.within(EB):
                    act.wait_ge(turned, t.b + 1)
                    if t.past(2):
                        act.wait_ge(lined, t.b - 1)
                    nc.scalar.activation(xT[:, t.slot, :], flat(ps_x), ACT.Copy).then_inc(copied, 1)
                    act.wait_ge(lined, t.b + 1)
                    if t.past(2):
                        act.wait_ge(mul2, t.b - 1)
                    nc.scalar.activation(xs[:, t.slot, :], flat(ps_l), ACT.Silu,
                                         bias=s["cols"][:, LIN_B:LIN_B + 1]).then_inc(active, 1)
                b = t.back(1)
                if b.within(EB):
                    act.wait_ge(product, b.b + 1)
                    if b.past(2):
                        act.wait_ge(scattered[b.slot], b.q * (16 * G))
                    nc.scalar.activation(res[:, b.slot, :, 0:H], ps_o1[:, :, :], ACT.Copy).then_inc(stored, 1)
                    nc.scalar.activation(res[:, b.slot, :, H:2 * H], ps_o2[:, :, :], ACT.Copy).then_inc(stored, 1)
            staggered(act, EB, 2, 4, 1, step)

        @block.vector
        def _(dve):
            def step(t):
                if t.within(EB):
                    if t.past(2):
                        dve.wait_ge(gathered[t.slot], t.q * (16 * G))
                    nc.vector.tensor_copy(src_idx[:, t.slot, :], s["src"][:, bass.ds(t.b * G, G)]).then_inc(idx_ready, 1)
                b = t.back(2)
                if b.within(EB):
                    if b.past(2):
                        dve.wait_ge(scattered[b.slot], b.q * (16 * G))
                    nc.vector.tensor_copy(dst_idx[:, b.slot, :],
                                          s["scat"][:, bass.ds(b.b * G, G)]).then_inc(dst_ready, 1)
                b = t.back(1)
                if b.within(EB):
                    prev = 1 - b.slot
                    dve.wait_ge(f_ready, b.b + 1)
                    dve.wait_ge(active, b.b + 1)
                    if b.past(1):
                        dve.wait_ge(scanned1, b.b)
                        dve.wait_ge(scanned2, b.b)
                    nc.vector.tensor_tensor(m1[:, :], flat(ps_f1), xs[:, b.slot, :], ALU.mult).then_inc(mul1, 1)
                    nc.vector.tensor_tensor(m2[:, :], flat(ps_f2), xs[:, b.slot, :], ALU.mult).then_inc(mul2, 1)
                    if b.past(2):
                        dve.wait_ge(product, b.b - 1)
                    for m, run, ready, done in ((m1, run1, mul1, scanned1), (m2, run2, mul2, scanned2)):
                        dve.wait_ge(ready, b.b + 1)
                        nc.vector.tensor_tensor_scan(run[:, b.slot, :], s["mask"][:, bass.ds(b.b * BLK, BLK)], m[:, :],
                                                     initial=run[:, prev, BLK - 1:BLK] if b.past(1) else 0.0,
                                                     op0=ALU.mult, op1=ALU.add).then_inc(done, 1)
            staggered(dve, EB, 2, 4, 2, step)


def nodes1(nc, tab, s, NB, LAST):
    with ExitStack() as ctx:
        def sb(name, shape, dt=F32):
            return ctx.enter_context(nc.sbuf_tensor(name, shape, dt))

        def ps(name):
            return ctx.enter_context(nc.psum_tensor(name, [P, G, P], F32))

        sem = phase_semaphores(nc, ctx, "nodes1")

        def flat(bank):
            return bank[:, :, :].rearrange("p j f -> p (j f)")

        def col(c):
            return s["cols"][:, c:c + 1]

        x, w = sb("n1_x", [P, 2, G, H]), sb("n1_w", [P, 2, G, 2 * H])
        xT, xx = sb("n1_xT", [P, 2, BLK]), sb("n1_xx", [P, 4, BLK])
        g1, g2 = sb("n1_g1", [P, 2, BLK]), sb("n1_g2", [P, 2, BLK])
        h1, h2 = sb("n1_h1", [P, 2, BLK]), sb("n1_h2", [P, 2, BLK])
        hs = [sb(f"n1_r{i}", [P, 2, BLK]) for i in range(4)]
        act_out = [sb(f"n1_s{i}", [P, BLK]) for i in range(3)]
        ps_x, ps_t, ps_l, ps_u1, ps_u2, ps_h, ps_ra, ps_rb = (ps(f"n1_ps{i}") for i in range(8))
        ps_r = (ps_ra, ps_rb, ps_ra)
        x_in, w_in, saved = ([sem(f"{n}{i}") for i in range(2)] for n in ("x_in", "w_in", "saved"))
        filled = sem("filled")
        (x_turned, x_copied, t1_turned, t2_turned, t1_copied, t2_copied, lined, active, u_done1, u_done2, pre1, pre2,
         h_ready1, h_ready2, cat_done, r0_ready, counted) = (sem(n) for n in (
             "x_turned", "x_copied", "t1_turned", "t2_turned", "t1_copied", "t2_copied", "lined", "active", "u_done1",
             "u_done2", "pre1", "pre2", "h_ready1", "h_ready2", "cat_done", "r0_ready", "counted"))
        r_done, r_act, r_added = ([sem(f"{n}{i}") for i in range(3)] for n in ("r_done", "r_act", "r_added"))
        x_v, w_v, d_v = rows_of(tab["x1"]), rows_of(tab["wide"]), rows_of(tab["last"])
        block = ctx.enter_context(nc.Block())

        @block.sync
        def _(sp):
            def step(t):
                if t.within(NB):
                    k = t.slot % 2
                    if t.past(2):
                        sp.wait_ge(x_turned, t.b - 1)
                    sp.dma_start(x[:, k], x_v[t.b]).then_inc(x_in[k], 16)
                    if t.past(2):
                        sp.wait_ge(t2_turned, t.b - 1)
                    sp.dma_start(w[:, k], w_v[t.b]).then_inc(w_in[k], 16)
                    sp.dma_start(d_v[t.b], s["default"][:, :, :]).then_inc(filled, 16)
            staggered(sp, NB, 4, 12, 0, step)
            sp.wait_ge(filled, 16 * NB)

        @block.tensor
        def _(pe):
            def residual(i, b):
                if b.within(NB):
                    if i == 0:
                        pe.wait_ge(r0_ready, b.b + 1)
                    else:
                        pe.wait_ge(r_added[i - 1], b.b + 1)
                    if i == 1 and b.past(1):
                        pe.wait_ge(r_act[1], b.b)
                    if i == 0 and b.past(3):
                        pe.wait_ge(r_act[2], b.b - 2)
                    if i == 2:
                        pe.wait_ge(r_act[0], (b.b + 3) if not isinstance(b.q, int) else min(b.b + 3, NB))
                        if isinstance(b.q, int) and b.past(1):
                            pe.wait_ge(r_act[2], b.b)
                    nc.tensor.matmul(flat(ps_r[i]), s["lins"][:, i, :], hs[i][:, b.slot % 2, :],
                                     start=True, stop=True).then_inc(r_done[i], 1)

            def step(t):
                d = t.back(1)
                if d.within(NB):
                    kd = d.slot % 2
                    pe.wait_ge(w_in[kd], d.round(2) * 16 + 16)
                    if d.past(1):
                        pe.wait_ge(t2_copied, d.b)
                    for j in range(G):
                        i = nc.tensor.transpose(ps_t[:, j, :], w[:, kd, j, 0:H], s["ident"][:, :])
                    i.then_inc(t1_turned, 1)
                residual(0, t.back(4))
                c = t.back(2)
                if c.within(NB):
                    pe.wait_ge(active, c.b + 1)
                    if c.past(1):
                        pe.wait_ge(pre1, c.b)
                    nc.tensor.matmul(flat(ps_u1), s["R1"][:, :], xx[:, c.slot, :],
                                     start=True, stop=True).then_inc(u_done1, 1)
                residual(1, t.back(5))
                if t.within(NB):
                    k = t.slot % 2
                    pe.wait_ge(x_in[k], t.round(2) * 16 + 16)
                    if t.past(1):
                        pe.wait_ge(x_copied, t.b)
                    for j in range(G):
                        i = nc.tensor.transpose(ps_x[:, j, :], x[:, k, j, :], s["ident"][:, :])
                    i.then_inc(x_turned, 1)
                if d.within(NB):
                    pe.wait_ge(t1_copied, d.b + 1)
                    for j in range(G):
                        i = nc.tensor.transpose(ps_t[:, j, :], w[:, kd, j, H:2 * H], s["ident"][:, :])
                    i.then_inc(t2_turned, 1)
                if c.within(NB):
                    if c.past(1):
                        pe.wait_ge(pre2, c.b)
                    nc.tensor.matmul(flat(ps_u2), s["R2"][:, :], xx[:, c.slot, :],
                                     start=True, stop=True).then_inc(u_done2, 1)
                residual(2, t.back(6))
                b = t.back(3)
                if b.within(NB):
                    pe.wait_ge(h_ready1, b.b + 1)
                    pe.wait_ge(h_ready2, b.b + 1)
                    if b.past(1):
                        pe.wait_ge(r0_ready, b.b)
                    nc.tensor.matmul(flat(ps_h), s["cat"][:, 0, :], h1[:, b.slot % 2, :], start=True, stop=False)
                    nc.tensor.matmul(flat(ps_h), s["cat"][:, 1, :], h2[:, b.slot % 2, :],
                                     start=False, stop=True).then_inc(cat_done, 1)
                b = t.back(1)
                if b.within(NB):
                    pe.wait_ge(x_copied, b.b + 1)
                    if b.past(1):
                        pe.wait_ge(active, b.b)
                    nc.tensor.matmul(flat(ps_l), s["lin"][:, :], xT[:, b.slot % 2, :],
                                     start=True, stop=True).then_inc(lined, 1)
            staggered(pe, NB, 4, 12, 6, step)

        @block.scalar
        def _(act):
            def residual(i, b):
                if b.within(NB):
                    act.wait_ge(r_done[i], b.b + 1)
                    if b.past(1):
                        act.wait_ge(r_added[i], b.b)
                    nc.scalar.activation(act_out[i][:, :], flat(ps_r[i]), ACT.Silu, bias=col(LS0 + i)).then_inc(r_act[i], 1)

            def step(t):
                b = t.back(7)
                if b.within(NB):
                    act.wait_ge(r_added[2], b.b + 1)
                    act.dma_start(tab["hT"][b.b], hs[3][:, b.slot % 2, :]).then_inc(saved[b.slot % 2], 16)
                k = t.slot % 2
                d = t.back(1)
                if d.within(NB):
                    act.wait_ge(t1_turned, d.b + 1)
                    if d.past(2):
                        act.wait_ge(h_ready1, d.b - 1)
                    nc.scalar.activation(g1[:, d.slot % 2, :], flat(ps_t), ACT.Copy).then_inc(t1_copied, 1)
                residual(0, t.back(4))
                residual(1, t.back(5))
                if t.within(NB):
                    act.wait_ge(x_turned, t.b + 1)
                    if t.past(2):
                        act.wait_ge(lined, t.b - 1)
                    nc.scalar.activation(xT[:, k, :], flat(ps_x), ACT.Copy).then_inc(x_copied, 1)
                c = t.back(2)
                if c.within(NB):
                    act.wait_ge(pre1, c.b + 1)
                    if c.past(2):
                        act.wait_ge(cat_done, c.b - 1)
                    nc.scalar.activation(h1[:, c.slot % 2, :], g1[:, c.slot % 2, :], ACT.Silu,
                                         bias=col(B1)).then_inc(h_ready1, 1)
                if d.within(NB):
                    act.wait_ge(t2_turned, d.b + 1)
                    if d.past(2):
                        act.wait_ge(h_ready2, d.b - 1)
                    nc.scalar.activation(g2[:, d.slot % 2, :], flat(ps_t), ACT.Copy).then_inc(t2_copied, 1)
                if c.within(NB):
                    act.wait_ge(pre2, c.b + 1)
                    nc.scalar.activation(h2[:, c.slot % 2, :], g2[:, c.slot % 2, :], ACT.Silu,
                                         bias=col(B2)).then_inc(h_ready2, 1)
                residual(2, t.back(6))
                b = t.back(1)
                if b.within(NB):
                    act.wait_ge(lined, b.b + 1)
                    if b.past(4):
                        act.wait_ge(r0_ready, b.b - 3)
                    nc.scalar.activation(xx[:, b.slot, :], flat(ps_l), ACT.Silu, bias=col(LIN_B)).then_inc(active, 1)
            staggered(act, NB, 4, 12, 7, step)
            for q in range(2):
                act.wait_ge(saved[q], 16 * NB // 2)

        @block.vector
        def _(dve):
            def step(t):
                b = t.back(4)
                if b.within(NB):
                    dve.wait_ge(r_act[0], b.b + 1)
                    if b.past(2):
                        dve.wait_ge(r_done[1], b.b - 1)
                        dve.wait_ge(r_added[1], b.b - 1)
                    nc.vector.tensor_tensor(hs[1][:, b.slot % 2, :], act_out[0][:, :], hs[0][:, b.slot % 2, :],
                                            ALU.add).then_inc(r_added[0], 1)
                c = t.back(2)
                if c.within(NB):
                    k = c.slot % 2
                    dve.wait_ge(u_done1, c.b + 1)
                    dve.wait_ge(t1_copied, c.b + 1)
                    nc.vector.tensor_tensor(g1[:, k, :], flat(ps_u1), g1[:, k, :], ALU.add).then_inc(pre1, 1)
                    dve.wait_ge(u_done2, c.b + 1)
                    dve.wait_ge(t2_copied, c.b + 1)
                    nc.vector.tensor_tensor(g2[:, k, :], flat(ps_u2), g2[:, k, :], ALU.add).then_inc(pre2, 1)
                b = t.back(3)
                if b.within(NB):
                    dve.wait_ge(cat_done, b.b + 1)
                    if b.past(2):
                        dve.wait_ge(r_added[0], b.b - 1)
                        dve.wait_ge(r_done[0], b.b - 1)
                    nc.vector.scalar_tensor_tensor(hs[0][:, b.slot % 2, :], flat(ps_h), col(CAT_B),
                                                   xx[:, b.slot, :], ALU.add, ALU.add).then_inc(r0_ready, 1)
                b = t.back(7)
                if b.within(NB):
                    dve.wait_ge(r_added[2], b.b + 1)
                    last = isinstance(b.q, int) and b.b == NB - 1
                    v = hs[3][:, b.slot % 2, :]
                    if last:
                        v = v.rearrange("f (j p) -> f j p", j=G)[:, :, 0:LAST // G]
                    nc.vector.bn_stats(s["stats"][:, b.b, :], v).then_inc(counted, 1)
            staggered(dve, NB, 4, 12, 7, step)

        @block.gpsimd
        def _(pool):
            def residual(i, b):
                if b.within(NB):
                    k = b.slot % 2
                    pool.wait_ge(r_act[i], b.b + 1)
                    if b.past(2):
                        if i == 2:
                            pool.wait_ge(saved[k], b.round(2) * 16)
                            pool.wait_ge(counted, b.b - 1)
                        else:
                            pool.wait_ge(r_done[i + 1], b.b - 1)
                            pool.wait_ge(r_added[i + 1], b.b - 1)
                    nc.gpsimd.tensor_tensor(hs[i + 1][:, k, :], act_out[i][:, :], hs[i][:, k, :],
                                            ALU.add).then_inc(r_added[i], 1)

            def step(t):
                residual(1, t.back(5))
                residual(2, t.back(6))
            staggered(pool, NB, 4, 12, 6, step)


def norm1(nc, tab, s, NB):
    with ExitStack() as ctx:
        def sb(name, shape, dt=F32):
            return ctx.enter_context(nc.sbuf_tensor(name, shape, dt))

        def ps(name):
            return [ctx.enter_context(nc.psum_tensor(f"{name}{i}", [P, G, P], F32)) for i in range(2)]

        sem = phase_semaphores(nc, ctx, "norm1")

        def col(c):
            return s["cols"][:, c:c + 1]

        small = sb("nm_small", [P, 16])
        shift = sb("nm_shift", [P, P])
        wn, row = sb("nm_w", [P, H]), sb("nm_row", [P, H])
        x, h = sb("nm_x", [P, 4, G, H]), sb("nm_h", [P, 2, BLK])
        v, o, xc = sb("nm_v", [P, 8, G, H]), sb("nm_o", [P, 4, G, H]), sb("nm_xc", [P, 2, G, H])
        ps_o = ps("nm_ps_o")
        ps_row = ctx.enter_context(nc.psum_tensor("nm_ps_row", [P, H], F32))
        ln = Norm(nc, ctx, sem, "nm_ln")
        x_in, h_in = [sem(f"x_in{i}") for i in range(4)], [sem(f"h_in{i}") for i in range(2)]
        saved = [sem(f"saved{i}") for i in range(4)]
        chain, var_ready, roots, shift_ready, row_product, weights, product, xc_ready, summed = (
            sem(n) for n in ("chain", "var_ready", "roots", "shift_ready", "row_product", "weights", "product",
                             "xc_ready", "summed"))
        x_v, o_v = rows_of(tab["x1"]), rows_of(tab["y2"])
        block = ctx.enter_context(nc.Block())
        MEAN, VAR, K, K2, V2, SD, SC, MSM, TV = range(9)

        def c1(i):
            return small[:, i:i + 1]

        @block.sync
        def _(sp):
            def step(t):
                if t.within(NB):
                    k = t.slot % 2
                    if t.past(4):
                        sp.wait_ge(xc_ready, t.b - 3)
                    sp.dma_start(x[:, t.slot % 4], x_v[t.b]).then_inc(x_in[t.slot % 4], 16)
                    if t.past(2):
                        sp.wait_ge(product, t.b - 1)
                    sp.dma_start(h[:, k], tab["hT"][t.b]).then_inc(h_in[k], 16)
            staggered(sp, NB, 8, 16, 0, step)

        @block.gpsimd
        def _(pool):
            def step(t):
                k = t.slot % 2
                pool.wait_ge(x_in[t.slot % 4], t.round(4) * 16 + 16)
                if t.past(2):
                    pool.wait_ge(summed, t.b - 1)
                nc.gpsimd.tensor_tensor(xc[:, k], x[:, t.slot % 4], to4(row), ALU.add).then_inc(xc_ready, 1)
            pool.wait_ge(weights, 2)
            staggered(pool, NB, 8, 16, 0, step)

        @block.tensor
        def _(pe):
            pe.wait_ge(shift_ready, 1)
            nc.tensor.matmul(ps_row[:, :], shift[:, :], s["fin"][:, :], start=True, stop=True).then_inc(row_product, 1)
            pe.wait_ge(weights, 1)

            def step(t):
                k = t.slot % 2
                pe.wait_ge(h_in[k], t.round(2) * 16 + 16)
                if t.past(2):
                    pe.wait_ge(summed, t.b - 1)
                for j in range(G):
                    i = nc.tensor.matmul(ps_o[k][:, j, :], h[:, k, tile(j)], wn[:, :], start=True, stop=True)
                i.then_inc(product, 1)
            staggered(pe, NB, 8, 16, 0, step)

        @block.vector
        def _(dve):
            wait_values = WaitValues(dve, "norm1_dve", 1)
            n = [0]

            def then(i):
                n[0] += 1
                i.then_inc(chain, 1)
                dve.wait_ge(chain, n[0])
            then(nc.vector.bn_aggr(small[:, MEAN:VAR + 1], s["stats"][:, :, :].rearrange("p b c -> p (b c)")))
            then(nc.vector.tensor_scalar(c1(K), col(NORM_MS), -1.0, 1.0, ALU.mult, ALU.add))
            then(nc.vector.tensor_tensor(c1(K), c1(K), c1(MEAN), ALU.mult))
            then(nc.vector.tensor_tensor(c1(K2), c1(K), c1(K), ALU.mult))
            nc.vector.tensor_tensor(c1(V2), c1(VAR), c1(K2), ALU.add).then_inc(var_ready, 1)
            dve.wait_ge(roots, 2)
            then(nc.vector.reciprocal(s["dis"][:, :], s["sdeg"][:, :]))
            then(nc.vector.reciprocal(c1(SC), c1(SD)))
            then(nc.vector.tensor_tensor(c1(SC), c1(SC), col(NORM_W), ALU.mult))
            nc.vector.tensor_scalar(wn[:, :], s["fin"][:, :], c1(SC), None, ALU.mult).then_inc(weights, 1)
            then(nc.vector.tensor_tensor(c1(MSM), c1(MEAN), col(NORM_MS), ALU.mult))
            then(nc.vector.tensor_tensor(c1(MSM), c1(MSM), c1(SC), ALU.mult))
            then(nc.vector.tensor_tensor(c1(TV), col(NORM_B), c1(MSM), ALU.subtract))
            nc.vector.tensor_scalar(shift[:, :], s["ident"][:, :], 0.0, c1(TV), ALU.mult, ALU.add).then_inc(shift_ready, 1)
            dve.wait_ge(row_product, 1)
            nc.vector.tensor_tensor(row[:, :], ps_row[:, :], s["finb"][:, :], ALU.add).then_inc(weights, 1)

            def step(t):
                b = t.back(4)
                if b.within(NB):
                    norm_inverse(nc, dve, ln, b.b, b.slot)
                if t.within(NB):
                    n, k = t.slot, t.slot % 2
                    dve.wait_ge(product, t.b + 1)
                    dve.wait_ge(xc_ready, t.b + 1)
                    if t.past(8):
                        dve.wait_ge(ln.applied, t.b - 7)
                    nc.vector.tensor_tensor(v[:, n], ps_o[k][:, :, :], xc[:, k], ALU.add).then_inc(summed, 1)
                b = t.back(2)
                if b.within(NB):
                    norm_moments(nc, dve, ln, wait_values, b.b, b.slot)
                b = t.back(4)
                if b.within(NB):
                    norm_times(nc, dve, ln, b.b, b.slot, s["dis"][:, bass.ds(b.b * G, G)])
                b = t.back(1)
                if b.within(NB):
                    n = b.slot
                    dve.wait_ge(summed, b.b + 1)
                    norm_stats(nc, ln, n, v[:, n])
                b = t.back(4)
                if b.within(NB):
                    norm_shift(nc, dve, ln, b.b, b.slot, steps=2)
            staggered(dve, NB, 8, 16, 4, step)

        @block.scalar
        def _(act):
            nc.scalar.activation(s["sdeg"][:, :], s["deg"][:, :], ACT.Sqrt).then_inc(roots, 1)
            act.wait_ge(var_ready, 1)
            nc.scalar.activation(c1(SD), c1(V2), ACT.Sqrt, bias=s["eps"][:, 0:1]).then_inc(roots, 1)

            def step(t):
                b = t.back(6)
                if b.within(NB):
                    act.wait_ge(ln.applied, b.b + 1)
                    act.dma_start(o_v[b.b], o[:, b.slot % 4]).then_inc(saved[b.slot % 4], 16)
                b = t.back(3)
                if b.within(NB):
                    norm_std(nc, act, ln, b.b, b.slot, s["eps"][:, 0:1])
                b = t.back(5)
                if b.within(NB):
                    k = b.slot % 4
                    if b.past(4):
                        act.wait_ge(saved[k], b.round(4) * 16)
                    norm_apply(nc, act, ln, b.b, b.slot, o[:, k], v[:, b.slot])
            staggered(act, NB, 8, 16, 6, step)
            for q in range(4):
                act.wait_ge(saved[q], 16 * NB // 4)


def edges2(nc, tab, s, EB):
    with ExitStack() as ctx:
        def sb(name, shape, dt=F32):
            return ctx.enter_context(nc.sbuf_tensor(name, shape, dt))

        def ps(name):
            return [ctx.enter_context(nc.psum_tensor(f"{name}{i}", [P, G, P], F32)) for i in range(2)]

        sem = phase_semaphores(nc, ctx, "edges2")

        src_idx, dst_idx = sb("e2_src_idx", [P, 2, G], I32), sb("e2_dst_idx", [P, 2, G], I32)
        rows = sb("e2_rows", [P, 2, G, H])
        run = sb("e2_run", [P, 2, BLK])
        res = sb("e2_res", [P, 2, G, TW])
        ps_x, ps_o = ps("e2_ps_x"), ps("e2_ps_o")
        gathered, scattered = [sem("gathered0"), sem("gathered1")], [sem("scattered0"), sem("scattered1")]
        idx_ready, dst_ready, turned, scanned, product, stored, cleared = (
            sem(n) for n in ("idx_ready", "dst_ready", "turned", "scanned", "product", "stored", "cleared"))
        block = ctx.enter_context(nc.Block())

        @block.gpsimd
        def _(pool):
            wait_values = WaitValues(pool, "edges2", 2)

            def step(t):
                if t.within(EB):
                    ready, freed = wait_values(t.b + 1, t.b - 1)
                    first_wait(pool, idx_ready)
                    pool.wait_ge(idx_ready, ready)
                    if t.past(2):
                        pool.wait_ge(turned, freed)
                    gather(nc, rows[:, t.slot], tab["y2"], src_idx[:, t.slot], gathered[t.slot])
                b = t.back(2)
                if b.within(EB):
                    ready, rows_ready = wait_values(b.b + 1, b.b + 1)
                    first_wait(pool, dst_ready)
                    pool.wait_ge(dst_ready, ready)
                    pool.wait_ge(stored, rows_ready)
                    scatter(nc, tab["narrow"], dst_idx[:, b.slot], res[:, b.slot], scattered[b.slot])
            nc.gpsimd.memset(res[:, :, :, :], 0.0).then_inc(cleared, 1)
            staggered(pool, EB, 2, 4, 2, step)
            for q in range(2):
                pool.wait_ge(scattered[q], 16 * G * EB // 2)

        @block.tensor
        def _(pe):
            def step(t):
                if t.within(EB):
                    pe.wait_ge(gathered[t.slot], t.q * (16 * G) + 16 * G)
                    if t.past(2):
                        pe.wait_ge(scanned, t.b - 1)
                    for j in range(G):
                        i = nc.tensor.transpose(ps_x[t.slot][:, j, :], rows[:, t.slot, j, :], s["ident"][:, :])
                    i.then_inc(turned, 1)
                b = t.back(1)
                if b.within(EB):
                    pe.wait_ge(scanned, b.b + 1)
                    if b.past(2):
                        pe.wait_ge(stored, b.b - 1)
                    for j in range(G):
                        i = nc.tensor.matmul(ps_o[b.slot][:, j, :], run[:, b.slot, tile(j)], s["w2"][:, :],
                                             start=True, stop=True)
                    i.then_inc(product, 1)
            staggered(pe, EB, 2, 4, 1, step)

        @block.vector
        def _(dve):
            def step(t):
                if t.within(EB):
                    if t.past(2):
                        dve.wait_ge(gathered[t.slot], t.q * (16 * G))
                    nc.vector.tensor_copy(src_idx[:, t.slot, :], s["src"][:, bass.ds(t.b * G, G)]).then_inc(idx_ready, 1)
                b = t.back(1)
                if b.within(EB):
                    if b.past(2):
                        dve.wait_ge(scattered[b.slot], b.q * (16 * G))
                        dve.wait_ge(product, b.b - 1)
                    nc.vector.tensor_copy(dst_idx[:, b.slot, :],
                                          s["scat"][:, bass.ds(b.b * G, G)]).then_inc(dst_ready, 1)
                    if b.past(1):
                        dve.wait_ge(scanned, b.b)
                    dve.wait_ge(turned, b.b + 1)
                    nc.vector.tensor_tensor_scan(run[:, b.slot, :], s["mask"][:, bass.ds(b.b * BLK, BLK)],
                                                 ps_x[b.slot][:, :, :].rearrange("p j f -> p (j f)"),
                                                 initial=run[:, 1 - b.slot, BLK - 1:BLK] if b.past(1) else 0.0,
                                                 op0=ALU.mult, op1=ALU.add).then_inc(scanned, 1)
            staggered(dve, EB, 2, 4, 1, step)

        @block.scalar
        def _(act):
            def step(t):
                act.wait_ge(product, t.b + 1)
                if t.past(2):
                    act.wait_ge(scattered[t.slot], t.q * (16 * G))
                nc.scalar.activation(res[:, t.slot, :, 0:H], ps_o[t.slot][:, :, :], ACT.Copy).then_inc(stored, 1)
            act.wait_ge(cleared, 1)
            staggered(act, EB, 2, 4, 0, step)


def nodes2(nc, tab, s, NB):
    with ExitStack() as ctx:
        def sb(name, shape, dt=F32):
            return ctx.enter_context(nc.sbuf_tensor(name, shape, dt))

        def ps(name):
            return [ctx.enter_context(nc.psum_tensor(f"{name}{i}", [P, G, P], F32)) for i in range(2)]

        sem = phase_semaphores(nc, ctx, "nodes2")

        y, w = sb("n2_y", [P, 4, G, H]), sb("n2_w", [P, 4, G, TW])
        yT = sb("n2_yT", [P, 2, BLK])
        x2 = sb("n2_x2", [P, 4, G, H])
        v, o = sb("n2_v", [P, 8, G, H]), sb("n2_o", [P, 4, G, H])
        ps_x, ps_o = ps("n2_ps_x"), ps("n2_ps_o")
        ln = Norm(nc, ctx, sem, "n2_ln")
        y_in, w_in = [sem(f"y_in{i}") for i in range(4)], [sem(f"w_in{i}") for i in range(4)]
        saved = [sem(f"saved{i}") for i in range(4)]
        turned, copied, product, rescaled, biased, summed = (
            sem(n) for n in ("turned", "copied", "product", "rescaled", "biased", "summed"))
        y_v, w_v, o_v = rows_of(tab["y2"]), rows_of(tab["narrow"]), rows_of(tab["x3"])
        block = ctx.enter_context(nc.Block())

        @block.sync
        def _(sp):
            def step(t):
                if t.within(NB):
                    if t.past(4):
                        sp.wait_ge(turned, t.b - 3)
                        sp.wait_ge(rescaled, t.b - 3)
                    sp.dma_start(y[:, t.slot % 4], y_v[t.b]).then_inc(y_in[t.slot % 4], 16)
                    if t.past(4):
                        sp.wait_ge(product, t.b - 3)
                    sp.dma_start(w[:, t.slot % 4], w_v[t.b]).then_inc(w_in[t.slot % 4], 16)
            staggered(sp, NB, 8, 16, 0, step)

        @block.gpsimd
        def _(pool):
            def step(t):
                pool.wait_ge(y_in[t.slot % 4], t.round(4) * 16 + 16)
                if t.past(4):
                    pool.wait_ge(summed, t.b - 3)
                nc.gpsimd.tensor_tensor(x2[:, t.slot % 4], y[:, t.slot % 4], per_node(s["sdeg"][:, bass.ds(t.b * G, G)]),
                                        ALU.mult).then_inc(rescaled, 1)
            staggered(pool, NB, 8, 16, 0, step)

        @block.tensor
        def _(pe):
            def step(t):
                if t.within(NB):
                    k = t.slot % 2
                    pe.wait_ge(y_in[t.slot % 4], t.round(4) * 16 + 16)
                    if t.past(2):
                        pe.wait_ge(copied, t.b - 1)
                    for j in range(G):
                        i = nc.tensor.transpose(ps_x[k][:, j, :], y[:, t.slot % 4, j, :], s["ident"][:, :])
                    i.then_inc(turned, 1)
                b = t.back(1)
                if b.within(NB):
                    k = b.slot % 2
                    pe.wait_ge(copied, b.b + 1)
                    pe.wait_ge(w_in[b.slot % 4], b.round(4) * 16 + 16)
                    if b.past(2):
                        pe.wait_ge(biased, b.b - 1)
                    for j in range(G):
                        nc.tensor.matmul(ps_o[k][:, j, :], yT[:, k, tile(j)], s["w2"][:, :], start=True, stop=False)
                        i = nc.tensor.matmul(ps_o[k][:, j, :], s["ident"][:, :], w[:, b.slot % 4, j, 0:H],
                                             start=False, stop=True)
                    i.then_inc(product, 1)
            staggered(pe, NB, 8, 16, 1, step)

        @block.vector
        def _(dve):
            wait_values = WaitValues(dve, "nodes2_dve", 1)
            def step(t):
                b = t.back(6)
                if b.within(NB):
                    norm_inverse(nc, dve, ln, b.b, b.slot)
                b = t.back(1)
                if b.within(NB):
                    k, n = b.slot % 2, b.slot
                    dve.wait_ge(product, b.b + 1)
                    if b.past(8):
                        dve.wait_ge(ln.applied, b.b - 7)
                    for j in range(G):
                        i = nc.vector.scalar_tensor_tensor(v[:, n, j, :], ps_o[k][:, j, :],
                                                           s["dis"][:, bass.ds(b.b * G + j, 1)], s["b2"][:, :],
                                                           ALU.mult, ALU.add)
                    i.then_inc(biased, 1)
                b = t.back(4)
                if b.within(NB):
                    norm_moments(nc, dve, ln, wait_values, b.b, b.slot)
                b = t.back(2)
                if b.within(NB):
                    n = b.slot
                    dve.wait_ge(biased, b.b + 1)
                    dve.wait_ge(rescaled, b.b + 1)
                    nc.vector.scalar_tensor_tensor(v[:, n], v[:, n], 0.0, x2[:, n % 4], ALU.max, ALU.add).then_inc(summed, 1)
                b = t.back(3)
                if b.within(NB):
                    n = b.slot
                    dve.wait_ge(summed, b.b + 1)
                    norm_stats(nc, ln, n, v[:, n])
                b = t.back(6)
                if b.within(NB):
                    norm_shift(nc, dve, ln, b.b, b.slot)
            staggered(dve, NB, 8, 16, 6, step)

        @block.scalar
        def _(act):
            def step(t):
                b = t.back(8)
                if b.within(NB):
                    act.wait_ge(ln.applied, b.b + 1)
                    act.dma_start(o_v[b.b], o[:, b.slot % 4]).then_inc(saved[b.slot % 4], 16)
                if t.within(NB):
                    k = t.slot % 2
                    act.wait_ge(turned, t.b + 1)
                    if t.past(2):
                        act.wait_ge(product, t.b - 1)
                    nc.scalar.activation(yT[:, k, :], ps_x[k][:, :, :].rearrange("p j f -> p (j f)"),
                                         ACT.Copy).then_inc(copied, 1)
                b = t.back(5)
                if b.within(NB):
                    norm_std(nc, act, ln, b.b, b.slot, s["eps"][:, 0:1])
                b = t.back(7)
                if b.within(NB):
                    k = b.slot % 4
                    if b.past(4):
                        act.wait_ge(saved[k], b.round(4) * 16)
                    norm_apply(nc, act, ln, b.b, b.slot, o[:, k], v[:, b.slot])
            staggered(act, NB, 8, 16, 8, step)
            for q in range(4):
                act.wait_ge(saved[q], 16 * NB // 4)


def edges3(nc, tab, s, EB):
    with ExitStack() as ctx:
        def sb(name, shape, dt=F32):
            return ctx.enter_context(nc.sbuf_tensor(name, shape, dt))

        def ps(name):
            return [ctx.enter_context(nc.psum_tensor(f"{name}{i}", [P, G, P], F32)) for i in range(2)]

        sem = phase_semaphores(nc, ctx, "edges3")

        src_idx, dst_idx = sb("e3_src_idx", [P, 2, G], I32), sb("e3_dst_idx", [P, 2, G], I32)
        rows, weighted = sb("e3_rows", [P, 2, G, H]), sb("e3_weighted", [P, 2, G, H])
        run = sb("e3_run", [P, 2, BLK])
        v, n = sb("e3_v", [P, 2, G, H]), sb("e3_n", [P, 2, G, H])
        res = sb("e3_res", [P, 2, G, H])
        ps_x, ps_o = ps("e3_ps_x"), ps("e3_ps_o")
        ln = Norm(nc, ctx, sem, "e3_ln")
        gathered, scattered = [sem("gathered0"), sem("gathered1")], [sem("scattered0"), sem("scattered1")]
        idx_ready, dst_ready, scaled, turned, scanned, product, biased, gained, shifted, stored = (
            sem(m) for m in ("idx_ready", "dst_ready", "scaled", "turned", "scanned", "product", "biased", "gained",
                             "shifted", "stored"))
        block = ctx.enter_context(nc.Block())

        @block.gpsimd
        def _(pool):
            wait_values = WaitValues(pool, "edges3", 2)

            def step(t):
                if t.within(EB):
                    ready, freed = wait_values(t.b + 1, t.b - 1)
                    first_wait(pool, idx_ready)
                    pool.wait_ge(idx_ready, ready)
                    if t.past(2):
                        pool.wait_ge(scaled, freed)
                    gather(nc, rows[:, t.slot], tab["x3"], src_idx[:, t.slot], gathered[t.slot])
                b = t.back(3)
                if b.within(EB):
                    ready, rows_ready = wait_values(b.b + 1, b.b + 1)
                    first_wait(pool, dst_ready)
                    pool.wait_ge(dst_ready, ready)
                    pool.wait_ge(stored, rows_ready)
                    scatter(nc, tab["last"], dst_idx[:, b.slot], res[:, b.slot], scattered[b.slot])
            staggered(pool, EB, 2, 6, 3, step)
            for q in range(2):
                pool.wait_ge(scattered[q], 16 * G * EB // 2)

        @block.tensor
        def _(pe):
            def step(t):
                if t.within(EB):
                    pe.wait_ge(scaled, t.b + 1)
                    if t.past(2):
                        pe.wait_ge(scanned, t.b - 1)
                    for j in range(G):
                        i = nc.tensor.transpose(ps_x[t.slot][:, j, :], weighted[:, t.slot, j, :], s["ident"][:, :])
                    i.then_inc(turned, 1)
                b = t.back(1)
                if b.within(EB):
                    pe.wait_ge(scanned, b.b + 1)
                    if b.past(2):
                        pe.wait_ge(biased, b.b - 1)
                    for j in range(G):
                        i = nc.tensor.matmul(ps_o[b.slot][:, j, :], run[:, b.slot, tile(j)], s["w3"][:, :],
                                             start=True, stop=True)
                    i.then_inc(product, 1)
            staggered(pe, EB, 2, 6, 1, step)

        @block.vector
        def _(dve):
            wait_values = WaitValues(dve, "edges3_dve", 1)
            def step(t):
                if t.within(EB):
                    if t.past(2):
                        dve.wait_ge(gathered[t.slot], t.q * (16 * G))
                    nc.vector.tensor_copy(src_idx[:, t.slot, :], s["src"][:, bass.ds(t.b * G, G)]).then_inc(idx_ready, 1)
                b = t.back(3)
                if b.within(EB):
                    k = b.slot
                    dve.wait_ge(ln.applied, b.b + 1)
                    nc.vector.tensor_tensor(n[:, k], n[:, k], to4(s["g3"]), ALU.mult).then_inc(gained, 1)
                    if b.past(2):
                        dve.wait_ge(scattered[k], b.q * (16 * G))
                    nc.vector.tensor_copy(dst_idx[:, k, :], s["scat"][:, bass.ds(b.b * G, G)]).then_inc(dst_ready, 1)
                    dve.wait_ge(gained, b.b + 1)
                    nc.vector.tensor_tensor(n[:, k], n[:, k], to4(s["be3"]), ALU.add).then_inc(shifted, 1)
                b = t.back(2)
                if b.within(EB):
                    k = b.slot
                    dve.wait_ge(product, b.b + 1)
                    if b.past(2):
                        dve.wait_ge(ln.applied, b.b - 1)
                    nc.vector.tensor_tensor(v[:, k], ps_o[k][:, :, :], to4(s["b3"]), ALU.add).then_inc(biased, 1)
                    dve.wait_ge(biased, b.b + 1)
                    norm_stats(nc, ln, k, v[:, k])
                b = t.back(1)
                if b.within(EB):
                    if b.past(1):
                        dve.wait_ge(scanned, b.b)
                    if b.past(2):
                        dve.wait_ge(product, b.b - 1)
                    dve.wait_ge(turned, b.b + 1)
                    nc.vector.tensor_tensor_scan(run[:, b.slot, :], s["mask"][:, bass.ds(b.b * BLK, BLK)],
                                                 ps_x[b.slot][:, :, :].rearrange("p j f -> p (j f)"),
                                                 initial=run[:, 1 - b.slot, BLK - 1:BLK] if b.past(1) else 0.0,
                                                 op0=ALU.mult, op1=ALU.add).then_inc(scanned, 1)
                b = t.back(2)
                if b.within(EB):
                    norm_moments(nc, dve, ln, wait_values, b.b, b.slot)
                if t.within(EB):
                    dve.wait_ge(gathered[t.slot], t.q * (16 * G) + 16 * G)
                    if t.past(2):
                        dve.wait_ge(turned, t.b - 1)
                    nc.vector.tensor_tensor(weighted[:, t.slot], rows[:, t.slot],
                                            per_node(s["ew"][:, bass.ds(t.b * G, G)]), ALU.mult).then_inc(scaled, 1)
                b = t.back(2)
                if b.within(EB):
                    norm_inverse(nc, dve, ln, b.b, b.slot)
                    norm_shift(nc, dve, ln, b.b, b.slot)
            staggered(dve, EB, 2, 6, 3, step)

        @block.scalar
        def _(act):
            def step(t):
                b = t.back(3)
                if b.within(EB):
                    k = b.slot
                    act.wait_ge(shifted, b.b + 1)
                    if b.past(2):
                        act.wait_ge(scattered[k], b.q * (16 * G))
                    nc.scalar.activation(res[:, k], n[:, k], ACT.Relu).then_inc(stored, 1)
                b = t.back(2)
                if b.within(EB):
                    k = b.slot
                    norm_std(nc, act, ln, b.b, k, s["eps"][:, 1:2])
                    norm_apply(nc, act, ln, b.b, k, n[:, k], v[:, k])
            staggered(act, EB, 2, 6, 3, step)


def nodes3(nc, tab, s, out, NB, LAST):
    with ExitStack() as ctx:
        def sb(name, shape, dt=F32):
            return ctx.enter_context(nc.sbuf_tensor(name, shape, dt))

        sem = phase_semaphores(nc, ctx, "nodes3")

        x, w = sb("n3_x", [P, 8, G, H]), sb("n3_w", [P, 8, G, H])
        v, o = sb("n3_v", [P, 8, G, H]), sb("n3_o", [P, 4, G, H])
        ln = Norm(nc, ctx, sem, "n3_ln")
        x_in, w_in = ([sem(f"{n}{i}") for i in range(8)] for n in ("x_in", "w_in"))
        saved = [sem(f"saved{i}") for i in range(4)]
        summed = sem("summed")
        x_v, w_v = rows_of(tab["x3"]), rows_of(tab["last"])
        o_v = rows_of(out[0:(NB - 1) * BLK, :])
        o_last = out[(NB - 1) * BLK:(NB - 1) * BLK + LAST, :].rearrange("(p j) f -> p j f", j=G)
        block = ctx.enter_context(nc.Block())

        @block.sync
        def _(sp):
            def step(t):
                if t.within(NB):
                    if t.past(8):
                        sp.wait_ge(summed, t.b - 7)
                    sp.dma_start(x[:, t.slot], x_v[t.b]).then_inc(x_in[t.slot], 16)
                    sp.dma_start(w[:, t.slot], w_v[t.b]).then_inc(w_in[t.slot], 16)
            staggered(sp, NB, 8, 16, 0, step)

        @block.gpsimd
        def _(pool):
            def step(t):
                pool.wait_ge(x_in[t.slot], t.round(8) * 16 + 16)
                pool.wait_ge(w_in[t.slot], t.round(8) * 16 + 16)
                if t.past(8):
                    pool.wait_ge(ln.applied, t.b - 7)
                nc.gpsimd.tensor_tensor(v[:, t.slot], x[:, t.slot], w[:, t.slot], ALU.add).then_inc(summed, 1)
            staggered(pool, NB, 8, 16, 0, step)

        @block.vector
        def _(dve):
            wait_values = WaitValues(dve, "nodes3_dve", 1)
            def step(t):
                b = t.back(4)
                if b.within(NB):
                    norm_inverse(nc, dve, ln, b.b, b.slot)
                b = t.back(2)
                if b.within(NB):
                    norm_moments(nc, dve, ln, wait_values, b.b, b.slot)
                b = t.back(1)
                if b.within(NB):
                    n = b.slot
                    dve.wait_ge(summed, b.b + 1)
                    norm_stats(nc, ln, n, v[:, n])
                b = t.back(4)
                if b.within(NB):
                    norm_shift(nc, dve, ln, b.b, b.slot)
            staggered(dve, NB, 8, 16, 4, step)

        @block.scalar
        def _(act):
            def step(t):
                b = t.back(6)
                if b.within(NB):
                    act.wait_ge(ln.applied, b.b + 1)
                    if isinstance(b.q, int) and b.b == NB - 1:
                        act.dma_start(o_last, o[0:LAST // G, b.slot % 4]).then_inc(saved[b.slot % 4], 16)
                    else:
                        act.dma_start(o_v[b.b], o[:, b.slot % 4]).then_inc(saved[b.slot % 4], 16)
                b = t.back(3)
                if b.within(NB):
                    norm_std(nc, act, ln, b.b, b.slot, s["eps"][:, 0:1])
                b = t.back(5)
                if b.within(NB):
                    k = b.slot % 4
                    if b.past(4):
                        act.wait_ge(saved[k], b.round(4) * 16)
                    norm_apply(nc, act, ln, b.b, b.slot, o[:, k], v[:, b.slot])
            staggered(act, NB, 8, 16, 6, step)
            for q in range(4):
                act.wait_ge(saved[q], 16 * NB // 4)


def layout(inputs):
    import numpy as np
    n, e = inputs["x"].shape[0], inputs["dst"].shape[0]
    nb = -(-n // (4 * BLK)) * 4
    eb = -(-e // (2 * BLK)) * 2
    pad_e = eb * BLK - e
    arrays = {k: np.ascontiguousarray(v) for k, v in inputs.items()}
    x = np.pad(arrays["x"], ((0, nb * BLK - n), (0, 0)))
    dst = np.concatenate([arrays["dst"], np.full(pad_e, n, arrays["dst"].dtype)])
    src = np.pad(arrays["src"], (0, pad_e))
    edge = np.array([-1], dst.dtype)
    nxt, prev = np.concatenate([dst[1:], edge]), np.concatenate([edge, dst[:-1]])

    def cols(v):
        return np.ascontiguousarray(v.reshape(-1, P).T)
    attr = np.concatenate([arrays["edge_attr_54"].T, arrays["edge_attr_18"].T])
    new = dict(
        x=x, dst_rows=dst, prev_rows=prev, dst_cols=cols(dst), next_cols=cols(nxt), src_cols=cols(src),
        edge_weight_cols=cols(np.pad(arrays["edge_weight"], (0, pad_e))), edge_attr_T=np.pad(attr, ((0, 0), (0, pad_e))),
        lin_T=arrays["L1_gnn_lin_W"].T, lin1_T=arrays["L1_gnn_lin1_W"].T, lin2_T=arrays["L1_gnn_lin2_W"].T,
        f1_W2_T=arrays["L1_gnn_f1_W2"].T, f2_W2_T=arrays["L1_gnn_f2_W2"].T, cat_T=arrays["L1_gnn_cat_W"].T,
        lins_T=arrays["L1_gnn_lins_W"].transpose(0, 2, 1), lins_b_T=arrays["L1_gnn_lins_b"].T,
        final_T=arrays["L1_gnn_final_W"].T)
    for k in AS_THEY_ARE:
        new[k] = arrays[k]
    return {k: np.ascontiguousarray(v) for k, v in new.items()}


AS_THEY_ARE = ["L0_gnn_W", "L0_gnn_b", "L1_gnn_lin_b", "L1_gnn_f1_W1", "L1_gnn_f2_W1", "L1_gnn_conv1_rel_W",
               "L1_gnn_conv1_rel_b", "L1_gnn_conv1_root_W", "L1_gnn_conv2_rel_W", "L1_gnn_conv2_rel_b",
               "L1_gnn_conv2_root_W", "L1_gnn_lin1_b", "L1_gnn_lin2_b", "L1_gnn_cat_b", "L1_gnn_norm_w",
               "L1_gnn_norm_b", "L1_gnn_norm_ms", "L1_gnn_final_b", "L2_gnn_W", "L2_gnn_b", "L3_gnn_W", "L3_gnn_b",
               "L3_gnn_gamma", "L3_gnn_beta"]


def kernel(**inputs):
    import concourse.bacc as bacc
    from concourse.bass_utils import run_bass_kernel_spmd

    arrays = layout(inputs)
    nc = bacc.Bacc("TRN2", target_bir_lowering=False, num_devices=1)
    a = {k: nc.dram_tensor(f"in_{k}", v.shape, mybir.dt.from_np(v.dtype), kind="ExternalInput").ap()
         for k, v in arrays.items()}
    n = inputs["x"].shape[0]
    out = nc.dram_tensor("out", (n, H), F32, kind="ExternalOutput").ap()
    build(nc, a, out, n)
    r = run_bass_kernel_spmd(nc, [{f"in_{k}": v for k, v in arrays.items()}], core_ids=[0])
    return r.results[0]["out"]
```
